# Optimizing a Trainium2 kernel written in Bass

```python
import numpy as np
import jax
import jax.numpy as jnp

def _softmax(x, axis=-1):
    return jax.nn.softmax(x, axis=axis)

def _gelu(x):
    return jax.nn.gelu(x, approximate=True)

def _silu(x):
    return jax.nn.silu(x)

def _sigmoid(x):
    return jax.nn.sigmoid(x)

def _layernorm(x, axis=-1, eps=1e-05):
    m = jnp.mean(x, axis=axis, keepdims=True)
    v = jnp.var(x, axis=axis, keepdims=True)
    return (x - m) / jnp.sqrt(v + eps)

def _scatter_add(tgt, idx, src, axis=0):
    return tgt.at[idx].add(src)

def _segment_sum(src, seg, n):
    return jax.ops.segment_sum(src, seg, n)
kernel_name = 'mk_gnn_ffn_d1_gnn_r8_a15924'

def setup_inputs(seed: int=0):
    np.random.seed(seed)
    _w = jnp.asarray

    def _rec_inputs():
        import jax
        import jax.numpy as jnp
        _gk = jax.random.key(seed)
        x = -0.0003713 + 1 * jax.random.normal(jax.random.fold_in(_gk, 1), (6250, 256), jnp.float32)
        src = jax.random.randint(jax.random.fold_in(_gk, 2), (100000,), 0, 6250, jnp.int32)
        dst = jnp.minimum((6250 * jax.random.uniform(jax.random.fold_in(_gk, 3), (100000,)) ** 2.0).astype(jnp.int32), 49999)
        _o = jnp.argsort(dst, stable=True)
        src = src[_o]
        dst = dst[_o]
        return (x, src, dst)
    x, src, dst = _rec_inputs()

    def _L0_gnn_setup():
        import jax, jax.numpy as jnp
        import numpy as np
        N_NODES = 6250
        N_EDGES = 100000
        D_IN = 256
        D_OUT = 256
        key = jax.random.key(seed)
        k_feat, k_src, k_dst, k_ws, k_wn, k_b = jax.random.split(key, 6)
        feat = jax.random.normal(k_feat, (N_NODES, D_IN), dtype=jnp.float32)
        src = jax.random.randint(k_src, (N_EDGES,), 0, N_NODES)
        dst = jax.random.randint(k_dst, (N_EDGES,), 0, N_NODES)
        scale = 1.0 / np.sqrt(D_IN)
        W_self = jax.random.normal(k_ws, (D_IN, D_OUT), dtype=jnp.float32) * scale
        W_neigh = jax.random.normal(k_wn, (D_IN, D_OUT), dtype=jnp.float32) * scale
        b = jnp.zeros((D_OUT,), dtype=jnp.float32)
        return {'feat': feat, 'W_self': W_self, 'W_neigh': W_neigh, 'b': b, 'src': src, 'dst': dst}
    _L0_gnn_all = _L0_gnn_setup()
    _L0_gnn_in = {k: v for k, v in _L0_gnn_all.items() if k in ('W_self', 'W_neigh', 'b')}
    del _L0_gnn_all

    def _L0_ffn_setup():
        import jax, jax.numpy as jnp
        import numpy as np
        E = 8
        K = 2
        D = 256
        H = 512
        DOUT = 256
        EPS = 1e-05
        key = jax.random.key(seed)
        ks = jax.random.split(key, 9)
        s = 0.02
        return {'x': jax.random.normal(ks[0], (4, 1024, D), jnp.float32), 'gamma': 1.0 + 0.05 * jax.random.normal(ks[1], (D,), jnp.float32), 'beta': 0.05 * jax.random.normal(ks[2], (D,), jnp.float32), 'Wr': 0.01 * jax.random.normal(ks[3], (D, E), jnp.float32), 'br': jnp.zeros((E,), jnp.float32), 'W1': s * jax.random.normal(ks[4], (E, D, H), jnp.float32), 'b1': s * jax.random.normal(ks[5], (E, H), jnp.float32), 'W2': s * jax.random.normal(ks[6], (E, H, DOUT), jnp.float32), 'b2': s * jax.random.normal(ks[7], (E, DOUT), jnp.float32)}
    _L0_ffn_all = _L0_ffn_setup()
    _L0_ffn_in = {k: v for k, v in _L0_ffn_all.items() if k in ('gamma', 'beta', 'Wr', 'br', 'W1', 'b1', 'W2', 'b2')}
    del _L0_ffn_all
    return {'x': x, 'src': src, 'dst': dst, 'L0_gnn_W_self': _L0_gnn_in['W_self'], 'L0_gnn_W_neigh': _L0_gnn_in['W_neigh'], 'L0_gnn_b': _L0_gnn_in['b'], 'L0_ffn_gamma': _L0_ffn_in['gamma'], 'L0_ffn_beta': _L0_ffn_in['beta'], 'L0_ffn_Wr': _L0_ffn_in['Wr'], 'L0_ffn_br': _L0_ffn_in['br'], 'L0_ffn_W1': _L0_ffn_in['W1'], 'L0_ffn_b1': _L0_ffn_in['b1'], 'L0_ffn_W2': _L0_ffn_in['W2'], 'L0_ffn_b2': _L0_ffn_in['b2']}

def reference(x, src, dst, L0_gnn_W_self, L0_gnn_W_neigh, L0_gnn_b, L0_ffn_gamma, L0_ffn_beta, L0_ffn_Wr, L0_ffn_br, L0_ffn_W1, L0_ffn_b1, L0_ffn_W2, L0_ffn_b2):
    import jax
    import jax.numpy as jnp

    def _L0_gnn_ref(feat, W_self, W_neigh, b, src, dst):
        import jax, jax.numpy as jnp
        import numpy as np
        N_NODES = 6250
        N_EDGES = 100000
        D_IN = 256
        D_OUT = 256
        n = feat.shape[0]
        msg = feat[src]
        agg = jax.ops.segment_sum(msg, dst, num_segments=n)
        deg = jax.ops.segment_sum(jnp.ones_like(dst, dtype=feat.dtype), dst, num_segments=n)
        h_neigh = agg / jnp.maximum(deg, 1.0)[:, None]
        out = feat @ W_self + h_neigh @ W_neigh + b
        return out

    def _L0_ffn_ref(x, gamma, beta, Wr, br, W1, b1, W2, b2):
        import jax, jax.numpy as jnp
        import numpy as np
        E = 8
        K = 2
        D = 256
        H = 512
        DOUT = 256
        EPS = 1e-05
        mu = jnp.mean(x, axis=-1, keepdims=True)
        var = jnp.mean(jnp.square(x - mu), axis=-1, keepdims=True)
        xn = (x - mu) * jax.lax.rsqrt(var + EPS) * gamma + beta
        logits = jnp.einsum('bsd,de->bse', xn, Wr) + br
        top_vals, top_idx = jax.lax.top_k(logits, K)
        w = jax.nn.softmax(top_vals, axis=-1)
        w_full = jnp.einsum('bsk,bske->bse', w, jax.nn.one_hot(top_idx, E, dtype=w.dtype))
        y = jnp.zeros(x.shape[:-1] + (DOUT,), x.dtype)
        for e in range(E):
            h = jax.nn.gelu(jnp.einsum('bsd,dh->bsh', xn, W1[e]) + b1[e], approximate=False)
            y_e = jnp.einsum('bsh,hd->bsd', h, W2[e]) + b2[e]
            y = y + y_e * w_full[..., e, None]
        return y
    x = x + _L0_gnn_ref(_layernorm(x, axis=-1), L0_gnn_W_self, L0_gnn_W_neigh, L0_gnn_b, src, dst)
    x = x + _L0_ffn_ref(_layernorm(x, axis=-1)[None], L0_ffn_gamma, L0_ffn_beta, L0_ffn_Wr, L0_ffn_br, L0_ffn_W1, L0_ffn_b1, L0_ffn_W2, L0_ffn_b2)[0]
    return x

_drawn_inputs = setup_inputs


def setup_inputs(seed=0):
    import zlib

    import numpy as np

    out = dict(_drawn_inputs(seed))
    spreads = {'L0_gnn_b': (0.0, 0.1), 'L0_ffn_br': (0.0, 0.1)}
    factors = {'L0_ffn_gamma': 8.0, 'L0_ffn_beta': 6.89, 'L0_ffn_b1': 8.0, 'L0_ffn_b2': 6.081}
    for name, (base, spread) in spreads.items():
        noise = np.random.default_rng([zlib.crc32(name.encode()), seed]).standard_normal(out[name].shape)
        drawn = base * np.exp(spread * noise) if base else spread * noise
        out[name] = jnp.asarray(drawn.astype(out[name].dtype))
    for name, factor in factors.items():
        out[name] = (out[name] * factor).astype(out[name].dtype)
    return out
```

```python
from contextlib import ExitStack

import concourse.bass as bass
from concourse import mybir

P = 128
F32 = mybir.dt.float32
I32 = mybir.dt.int32
ALU = mybir.AluOpType
ACT = mybir.ActivationFunctionType
AX = mybir.AxisListType
EPS = 1e-5

GT = 4
GS = 4
LC = 7
XS = 3
LOWEST = -3.0e38


def build(nc, x, src, dst, w_self, w_neigh, b_gnn, gamma, beta, w_r, b_r, w1, b1, w2, b2, out):
    NP, D = x.shape
    NB = NP // P
    NT = src.shape[1]
    NG = NT // GT
    NI = NG // GS
    DK = D // P
    NE, _, H = w1.shape
    HK = H // P
    R = D + 2
    NJ = (2 * NP + NE * (P - 1)) // P
    LC_N = NB // LC
    assert NB % LC == 0 and NG % GS == 0 and NI == NB and NJ % XS == 0 and NB * NE <= 512

    table = nc.dram_tensor("feature_table", [NP, D], F32, kind="Internal").ap()
    slots = nc.dram_tensor("slot_rows", [NJ * P, R], F32, kind="Internal").ap()

    with ExitStack() as ctx:
        def sb(name, shape, dt=F32):
            return ctx.enter_context(nc.sbuf_tensor(name, shape, dt))

        def sem(name):
            return ctx.enter_context(nc.semaphore(name))

        bank = [ctx.enter_context(nc.psum_tensor(f"bank{i}", [P, 512], F32)) for i in range(8)]

        res = sb("res", [P, NB, D])
        w2_sb = res[:, :, :].rearrange("p b d -> p (b d)")[:, 0:HK * NE * D].rearrange("p (k e d) -> p k e d", k=HK, e=NE)
        WF = max(NB * D, NE * DK * H + NE * H)
        feat_region = sb("feat_region", [P, WF])
        feat = feat_region[:, 0:NB * D].rearrange("p (b d) -> p b d", d=D)
        w1_sb = feat_region[:, 0:NE * DK * H].rearrange("p (k e h) -> p k e h", k=DK, e=NE)
        b1_sb = feat_region[:, NE * DK * H:NE * DK * H + NE * H].rearrange("p (e h) -> p e h", e=NE)
        agg = sb("agg", [P, NB + 1, R])
        ring = sb("ring", [P, GS * GT, R])
        pool_a = ring[:, :, :].rearrange("p a r -> p (a r)")
        onehot = sb("onehot", [P, GS, GT, P])
        onehot_flat = onehot[:, :, :, :].rearrange("p a b c -> p (a b c)")
        ws_sb = sb("ws_sb", [P, DK, D])
        wn_sb = sb("wn_sb", [P, DK, D])
        bg_sb = sb("bg_sb", [1, D])
        wr_sb = sb("wr_sb", [P, DK, NE])
        br_sb = sb("br_sb", [P, NE])
        gb_sb = sb("gb_sb", [P, 2, DK])
        ident = sb("ident", [P, P])
        upper = sb("upper", [P, P])
        ones = sb("ones", [P, P])
        zrow = sb("zrow", [P, 1, R])
        iota = sb("iota", [P, P])
        iota_p = sb("iota_p", [P, 1])
        node_no = sb("node_no", [P, NB])
        src_sb = sb("src_sb", [P, NT], I32)
        idx = sb("idx", [P, GS, GT], I32)
        dst_i = sb("dst_i", [P, NT], I32)
        inside = sb("inside", [P, NT])
        target = sb("target", [P, NT])
        missed = sb("missed", [P, NT])
        base_i = sb("base_i", [P, NG], I32)
        block_i = sb("block_i", [1, NG], I32)
        in_first = sb("in_first", [P, NG])
        base_f = in_first[0:1, :]
        in_second = sb("in_second", [P, NG])
        n_missed = sb("n_missed", [P, 2])
        missed_i = sb("missed_i", [1, 1], I32)
        stats = sb("stats", [P, NB, 6])
        mv = sb("mv", [P, NB, 2])
        rstd = sb("rstd", [P, NB])
        nmr = sb("nmr", [P, NB])
        stage = [sb("stage", [P, D]), onehot_flat[:, 2 * D:3 * D]]
        stage_t = [onehot_flat[:, s * D:(s + 1) * D].rearrange("p (k t) -> p k t", k=DK) for s in range(2)]
        stage_f = sb("stage_f", [P, DK, P])
        expert_i = sb("expert_i", [1, NJ], I32)

        BE = NB * NE
        assert 2 * BE <= NT

        def be(t, n):
            return t[:, n * BE:(n + 1) * BE].rearrange("p (b e) -> p b e", e=NE)

        edge_f = target
        logits, choice1 = be(inside, 0), be(inside, 1)
        choice2, work = be(target, 0), be(target, 1)
        both, total = be(missed, 0), be(missed, 1)
        incl = sb("incl", [P, NB, NE])
        stats_flat = stats[:, :, :].rearrange("p b s -> p (b s)")
        v1 = stats_flat[:, 2 * NB:3 * NB]
        v2 = sb("v2", [P, NB])
        i1 = stats_flat[:, 3 * NB:4 * NB]
        p1 = sb("p1", [P, NB])
        p2 = sb("p2", [P, NB])
        slot_f = stats_flat[:, 0:2 * NB].rearrange("p (k b) -> p k b", k=2)
        slot_i = sb("slot_i", [P, 2, NB], I32)
        tiles_i = sb("tiles_i", [P, NE], I32)
        tiles_f = sb("tiles_f", [P, NE])
        tiles_c = sb("tiles_c", [P, NE])
        offset = sb("offset", [P, NE])
        reach = onehot_flat[0:1, 0:NJ * NE].rearrange("p (j e) -> p j e", e=NE)
        iota_j = sb("iota_j", [1, NJ])
        expert_f = in_first[0:1, 0:NJ]

        b2_sb = pool_a[:, 0:NE * D].rearrange("p (e d) -> p e d", e=NE)
        row = [agg[:, s, :] for s in range(XS)]
        y_out = [agg[:, XS + s, 0:D] for s in range(XS)]
        xt = [agg[:, 2 * XS + s, 0:D].rearrange("p (k t) -> p k t", k=DK) for s in range(XS)]
        row_tail = [sb(f"row_tail{s}", [P, R - D]) for s in range(XS)]
        row_id = [sb(f"row_id{s}", [P, 1], I32) for s in range(XS)]
        hid = pool_a[:, NE * D:NE * D + H]
        ht = pool_a[:, NE * D + H:NE * D + 2 * H].rearrange("p (k t) -> p k t", k=HK)
        assert NE * D + 2 * H <= GS * GT * R and 3 * XS <= NB

        small_in = sem("small_in")
        dst_in = sem("dst_in")
        src_in = sem("src_in")
        x_in = [sem(f"x_in{c}") for c in range(LC_N)]
        w2_in = sem("w2_in")
        w1_in = sem("w1_in")
        b2_in = sem("b2_in")
        consts = sem("consts")
        zeroed = sem("zeroed")
        agg_zero = sem("agg_zero")
        ring_ones = sem("ring_ones")
        var_ready = sem("var_ready")
        root_ready = sem("root_ready")
        stats_ready = sem("stats_ready")
        feat_ready = sem("feat_ready")
        table_out = sem("table_out")
        slots_zero = sem("slots_zero")
        base_ready = sem("base_ready")
        base_bc = sem("base_bc")
        miss_sum = sem("miss_sum")
        miss_bc = sem("miss_bc")
        miss_ready = sem("miss_ready")
        idx_ready = sem("idx_ready")
        gathered = [sem(f"gathered{q}") for q in range(GS)]
        hot_ready = sem("hot_ready")
        summed = [sem(f"summed{q}") for q in range(GS)]
        added = [sem(f"added{q}") for q in range(GS)]
        f_staged = sem("f_staged")
        f_turned = sem("f_turned")
        f_copied = sem("f_copied")
        f_product = sem("f_product")
        res_added = sem("res_added")
        m_idx = sem("m_idx")
        m_gathered = sem("m_gathered")
        m_hot = sem("m_hot")
        m_sum = sem("m_sum")
        m_add = sem("m_add")
        deg_ready = sem("deg_ready")
        n_staged = [sem(f"n_staged{s}") for s in range(2)]
        n_turned = [sem(f"n_turned{s}") for s in range(2)]
        n_copied = [sem(f"n_copied{s}") for s in range(2)]
        n_product = [sem(f"n_product{s}") for s in range(2)]
        x1_ready = [sem(f"x1_ready{s}") for s in range(2)]
        st1_ready = sem("st1_ready")
        z_ready = sem("z_ready")
        st2_ready = sem("st2_ready")
        xn_ready = sem("xn_ready")
        r_staged = [sem(f"r_staged{s}") for s in range(2)]
        r_turned = [sem(f"r_turned{s}") for s in range(2)]
        r_copied = [sem(f"r_copied{s}") for s in range(2)]
        r_product = [sem(f"r_product{s}") for s in range(2)]
        logit_ready = [sem(f"logit_ready{s}") for s in range(2)]
        x1_out = sem("x1_out")
        chosen = sem("chosen")
        counted = sem("counted")
        plan_ready = sem("plan_ready")
        scattered = sem("scattered")
        p2_set = sem("p2_set")
        row_in = [sem(f"row_in{s}") for s in range(XS)]
        row_free = sem("row_free")
        t_done = sem("t_done")
        xt_ready = sem("xt_ready")
        h_done = sem("h_done")
        h_biased = sem("h_biased")
        gelu_done = sem("gelu_done")
        gt_done = sem("gt_done")
        ht_ready = sem("ht_ready")
        y_done = sem("y_done")
        y_ready = sem("y_ready")
        y_free = sem("y_free")
        y_biased = sem("y_biased")
        y_added = sem("y_added")
        chain = sem("chain")
        gate = sem("gate")
        gate_pe = sem("gate_pe")
        gate_act = sem("gate_act")

        block = ctx.enter_context(nc.Block())

        def rows(t):
            return t.rearrange("(b p) d -> p b d", p=P)

        x_v, table_v, out_v = rows(x), rows(table), rows(out[0:NP, :])
        slots_v = slots.rearrange("(j p) r -> j p r", p=P)

        @block.sync
        def _(sp):
            sp.dma_start(dst_i[:, :], dst).then_inc(dst_in, 16)
            for c in range(LC_N):
                s = slice(c * LC, (c + 1) * LC)
                sp.dma_start(res[:, s, :], x_v[:, s, :]).then_inc(x_in[c], 16)
            sp.dma_start(src_sb[:, :], src).then_inc(src_in, 16)
            sp.dma_start(ws_sb[:, :, :], w_self.rearrange("(k p) n -> p k n", p=P)).then_inc(small_in, 16)
            sp.dma_start(wn_sb[:, :, :], w_neigh.rearrange("(k p) n -> p k n", p=P)).then_inc(small_in, 16)
            sp.dma_start(bg_sb[:, :], b_gnn).then_inc(small_in, 16)
            sp.dma_start(wr_sb[:, :, :], w_r.rearrange("(k p) n -> p k n", p=P)).then_inc(small_in, 16)
            sp.dma_start(br_sb[:, :], b_r.broadcast_to([P, NE])).then_inc(small_in, 16)
            sp.dma_start(gb_sb[:, 0, :], gamma).then_inc(small_in, 16)
            sp.dma_start(gb_sb[:, 1, :], beta).then_inc(small_in, 16)
            for c in range(LC_N):
                s = slice(c * LC, (c + 1) * LC)
                sp.wait_ge(feat_ready, (c + 1) * LC)
                sp.dma_start(table_v[:, s, :], feat[:, s, :]).then_inc(table_out, 16)
            sp.wait_ge(zeroed, 3)
            NZ = NJ // 7
            for c in range(7):
                sp.dma_start(slots.rearrange("(c j p) r -> c p j r", p=P, c=7)[c],
                             zrow[:, :, :].broadcast_to([P, NZ, R])).then_inc(slots_zero, 16)
            sp.wait_ge(f_staged, NB)
            sp.wait_ge(table_out, 16 * LC_N)
            for k in range(DK):
                sp.dma_start(w1_sb[:, k, :, :], w1[:, k * P:(k + 1) * P, :].rearrange("e p h -> p e h")).then_inc(w1_in, 16)
            sp.dma_start(b1_sb, b1.broadcast_to([P, NE * H]).rearrange("p (e h) -> p e h", e=NE)).then_inc(w1_in, 16)
            sp.wait_ge(deg_ready, 1)
            sp.dma_start(b2_sb, b2.broadcast_to([P, NE * D]).rearrange("p (e d) -> p e d", e=NE)).then_inc(b2_in, 16)
            sp.dma_start(out[NP:NP + P, :], zrow[:, 0, 0:D]).then_inc(x1_out, 16)
            sp.wait_ge(st1_ready, NB + 1)
            for c in range(LC_N):
                s = slice(c * LC, (c + 1) * LC)
                sp.dma_start(out_v[:, s, :], res[:, s, :]).then_inc(x1_out, 16)
            sp.wait_ge(z_ready, NB)
            sp.wait_ge(x1_out, 16 * (LC_N + 1))
            for k in range(HK):
                sp.dma_start(w2_sb[:, k, :, :], w2[:, k * P:(k + 1) * P, :].rearrange("e p d -> p e d")).then_inc(w2_in, 16)
            sp.wait_ge(scattered, 2 * 16 * NB)
            def load_row(j, s):
                sp.dma_start(row[s], slots_v[bass.ds(j, 1), :, :].rearrange("o p r -> (o p) r")).then_inc(row_in[s], 16)

            for s in range(XS):
                load_row(s, s)
            with sp.Fori(1, NJ // XS) as i:
                for s in range(XS):
                    sp.wait_ge(row_free, XS * i + s - XS + 1)
                    load_row(XS * i + s, s)
            for s in range(XS):
                sp.wait_ge(row_in[s], 16 * (NJ // XS))
            sp.wait_ge(y_added, 16 * NJ)

        @block.gpsimd
        def _(pool):
            pool.memset(ones[:, :], 1.0).then_inc(consts, 1)
            pool.iota(iota[:, :], [[1, P]], base=0, channel_multiplier=0, allow_small_or_imprecise_dtypes=True).then_inc(consts, 1)
            pool.iota(iota_p[:, :], [[0, 1]], base=0, channel_multiplier=1, allow_small_or_imprecise_dtypes=True).then_inc(consts, 1)
            pool.iota(node_no[:, :], [[P, NB]], base=0, channel_multiplier=1, allow_small_or_imprecise_dtypes=True).then_inc(consts, 1)
            pool.iota(iota_j[:, :], [[1, NJ]], base=0, channel_multiplier=0, allow_small_or_imprecise_dtypes=True).then_inc(consts, 1)
            pool.wait_ge(consts, 1)
            pool.affine_select(out=ident[:, :], in_=ones[:, :], compare_op=ALU.is_equal, fill=0.0,
                               base=0, pattern=[[-1, P]], channel_multiplier=1).then_inc(consts, 1)
            pool.affine_select(out=upper[:, :], in_=ones[:, :], compare_op=ALU.is_gt, fill=0.0,
                               base=0, pattern=[[1, P]], channel_multiplier=-1).then_inc(consts, 1)
            pool.memset(zrow[:, :, 0:D + 1], 0.0).then_inc(zeroed, 1)
            pool.iota(zrow[:, 0, D + 1:R], [[0, 1]], base=NP, channel_multiplier=1, allow_small_or_imprecise_dtypes=True).then_inc(zeroed, 1)
            pool.memset(ring[:, :, D:D + 1], 1.0).then_inc(ring_ones, 1)
            pool.memset(agg[:, :, :], 0.0).then_inc(agg_zero, 1)
            pool.wait_ge(agg_zero, 1)
            pool.sem_inc(zeroed, 1)
            pool.wait_ge(table_out, 16 * LC_N)
            with pool.Fori(0, NI) as i:
                for q in range(GS):
                    pool.wait_ge(idx_ready, GS * i + q + 1)
                    pool.wait_ge(summed[q], i + 1)
                    pool.sem_inc(gate, 1)
                    for t in range(GT):
                        pool.indirect_dma_start(ring[:, q * GT + t, 0:D], None, table,
                                                bass.IndirectOffsetOnAxis(idx[:, q, t:t + 1], 0)).then_inc(gathered[q], 16)
            pool.wait_ge(miss_ready, 1)
            n_miss = pool.value_load(missed_i[0:1, 0:1], min_val=0, max_val=NT * P)
            for q in range(GS):
                pool.wait_ge(summed[q], NI + 1)
            with pool.If(n_miss > 0):
                with pool.Fori(0, NT) as t:
                    pool.wait_ge(m_sum, NB * t + 1)
                    pool.tensor_copy(idx[:, 0, 0:1], src_sb[:, bass.ds(t, 1)]).then_inc(m_idx, 1)
                    pool.wait_ge(m_idx, t + 1)
                    pool.sem_inc(gate, 1)
                    pool.indirect_dma_start(ring[:, 0, 0:D], None, table,
                                            bass.IndirectOffsetOnAxis(idx[:, 0, 0:1], 0)).then_inc(m_gathered, 16)
            def staged(b, n, s):
                pool.wait_ge(xn_ready, b + 1)
                pool.wait_ge(r_turned[s], n + 1)
                pool.sem_inc(gate, 1)
                pool.tensor_copy(stage[s][:, :], agg[:, bass.ds(b, 1), 0:D].rearrange("p o d -> p (o d)")).then_inc(r_staged[s], 1)

            staged(0, 0, 0)
            with pool.Fori(0, NB // 2) as i:
                staged(2 * i + 1, i, 1)
                staged(2 * i + 2, i + 1, 0)
            pool.wait_ge(plan_ready, 1)
            pool.wait_ge(slots_zero, 16 * 7)
            for k in range(2):
                if k == 1:
                    pool.wait_ge(p2_set, 1)
                for b in range(NB):
                    pool.indirect_dma_start(slots, bass.IndirectOffsetOnAxis(slot_i[:, k, b:b + 1], 0),
                                            agg[:, b, :], None).then_inc(scattered, 16)
            pool.wait_ge(x1_out, 16 * (LC_N + 1))

            def add_rows(j, s):
                pool.wait_ge(y_ready, j + 1)
                pool.sem_inc(gate, 1)
                pool.indirect_dma_start(out, bass.IndirectOffsetOnAxis(row_id[s][:, :], 0),
                                        y_out[s], None, compute_op=ALU.add).then_inc(y_added, 16)

            def added_before(j):
                pool.wait_ge(y_added, 16 * j)
                pool.sem_inc(y_free, 1)

            add_rows(0, 0)
            for j in range(1, XS):
                added_before(j)
                add_rows(j, j)
            with pool.Fori(1, NJ // XS) as i:
                for s in range(XS):
                    added_before(XS * i + s)
                    add_rows(XS * i + s, s)

        @block.scalar
        def _(act):
            def root(lo, hi, n):
                act.wait_ge(var_ready, n)
                act.activation(rstd[:, lo:hi], rstd[:, lo:hi], ACT.Sqrt).then_inc(root_ready, 1)

            for s in (f_copied, *n_copied):
                act.sem_inc(s, 1)
            for c in range(LC_N):
                root(c * LC, (c + 1) * LC, c + 1)
                act.wait_ge(stats_ready, c + 1)
                for b in range(c * LC, (c + 1) * LC):
                    act.activation(feat[:, b, :], res[:, b, :], ACT.Identity, bias=nmr[:, b:b + 1],
                                   scale=rstd[:, b:b + 1]).then_inc(feat_ready, 1)
            act.wait_ge(feat_ready, NB)
            act.wait_ge(src_in, 16)
            with act.Fori(0, NI) as i:
                for q in range(GS):
                    act.wait_ge(summed[q], i + 1)
                    act.copy(idx[:, q, :], src_sb[:, bass.ds(i * GS * GT + q * GT, GT)]).then_inc(idx_ready, 1)
                    if q == 0:
                        act.wait_ge(f_turned, i + 1)
                        act.copy(stage[0][:, :], feat[:, bass.ds(i, 1), :]).then_inc(f_staged, 1)
                    if q == 1:
                        act.wait_ge(f_turned, i + 2)
                        act.wait_ge(f_product, i + 1)
                        act.copy(stage_f[:, :, :], bank[4][:, 0:D].rearrange("p (k t) -> p k t", k=DK)).then_inc(f_copied, 1)
            act.wait_ge(deg_ready, 1)
            act.wait_ge(f_product, NB + 1)

            def mean(b, n, s):
                act.wait_ge(n_turned[s], n + 1)
                act.activation(stage[s][:, :], agg[:, bass.ds(b, 1), 0:D], ACT.Copy, scale=rstd[:, bass.ds(b, 1)]).then_inc(n_staged[s], 1)

            def mean_turned(n, s):
                act.wait_ge(n_turned[s], n + 2)
                act.wait_ge(n_product[s], n + 1)
                act.copy(stage_t[s], bank[s][:, 0:D].rearrange("p (k t) -> p k t", k=DK)).then_inc(n_copied[s], 1)

            mean(0, 0, 0)
            with act.Fori(0, NB // 2) as i:
                mean(2 * i + 1, i, 1)
                mean_turned(i, 0)
                mean(2 * i + 2, i + 1, 0)
                mean_turned(i, 1)
            mean_turned(NB // 2, 0)
            root(0, NB, LC_N + 1)
            act.wait_ge(st1_ready, NB + 1)
            with act.Fori(0, NB) as b:
                act.activation(agg[:, bass.ds(b, 1), 0:D], res[:, bass.ds(b, 1), :], ACT.Identity,
                               bias=nmr[:, bass.ds(b, 1)], scale=rstd[:, bass.ds(b, 1)]).then_inc(z_ready, 1)
            root(0, NB, LC_N + 2)

            act.wait_ge(st2_ready, NB + 1)
            with act.Fori(0, NB) as b:
                z = agg[:, bass.ds(b, 1), 0:D]
                act.activation(z, z, ACT.Identity, bias=nmr[:, bass.ds(b, 1)], scale=rstd[:, bass.ds(b, 1)]).then_inc(xn_ready, 1)
            act.wait_ge(chosen, 1)
            act.activation(p2[:, :], v2[:, :], ACT.Exp).then_inc(chosen, 1)
            act.wait_ge(plan_ready, 1)

            def gelu(j):
                act.wait_ge(h_biased, j + 1)
                act.activation(hid, hid, ACT.Gelu).then_inc(gelu_done, 1)

            def hidden_turned(j):
                act.wait_ge(gt_done, j + 1)
                if not isinstance(j, int) or j > 0:
                    act.wait_ge(y_done, j)
                act.copy(ht, bank[2][:, :].rearrange("p (k t) -> p k t", k=HK)).then_inc(ht_ready, 1)

            gelu(0)
            hidden_turned(0)
            with act.Fori(1, NJ) as j:
                gelu(j)
                hidden_turned(j)

        @block.tensor
        def _(pe):
            for s in (*summed, f_turned, f_product, m_sum, *n_turned, *n_product, *r_turned, *r_product):
                pe.sem_inc(s, 1)
            pe.wait_ge(consts, 7)
            pe.wait_ge(base_ready, 1)
            pe.matmul(bank[6][:, 0:NG], ones[0:1, :], base_f, start=True, stop=True).then_inc(base_bc, 1)
            pe.wait_ge(miss_sum, 1)
            pe.matmul(bank[7][0:1, 0:1], n_missed[:, 0:1], ones[:, 0:1], start=True, stop=True).then_inc(miss_bc, 1)
            pe.wait_ge(small_in, 16 * 7)
            pe.wait_ge(ring_ones, 1)

            def turn(to, block):
                for k in range(DK):
                    last = pe.transpose(to[:, k * P:(k + 1) * P], block[:, k * P:(k + 1) * P], ident[:, :])
                return last

            with pe.Fori(0, NI) as i:
                for q in range(GS):
                    pe.wait_ge(hot_ready, GS * i + q + 1)
                    pe.wait_ge(gathered[q], 16 * GT * (i + 1))
                    pe.wait_ge(added[q], i + 1)
                    for t in range(GT):
                        last = pe.matmul(bank[q][:, 0:D + 1], onehot[:, q, t, :], ring[:, q * GT + t, 0:D + 1],
                                         start=(t == 0), stop=(t == GT - 1))
                    last.then_inc(summed[q], 1)
                    if q == 0:
                        pe.wait_ge(f_staged, i + 1)
                        pe.wait_ge(f_copied, i + 1)
                        turn(bank[4], stage[0]).then_inc(f_turned, 1)
                    if q == 2:
                        pe.wait_ge(f_copied, i + 2)
                        pe.wait_ge(res_added, i + 1)
                        for k in range(DK):
                            pe.matmul(bank[5][:, 0:D], stage_f[:, k, :], ws_sb[:, k, :], start=(k == 0), stop=False)
                        pe.matmul(bank[5][:, 0:D], ones[0:1, :], bg_sb[:, :], start=False, stop=True).then_inc(f_product, 1)
            pe.wait_ge(miss_ready, 1)
            n_miss = pe.value_load(missed_i[0:1, 0:1], min_val=0, max_val=NT * P)
            with pe.If(n_miss > 0):
                with pe.Fori(0, NT) as t:
                    pe.wait_ge(m_gathered, 16 * (t + 1))
                    pe.sem_inc(gate_pe, 1)
                    with pe.Fori(0, NB) as w:
                        pe.wait_ge(m_hot, NB * t + w + 1)
                        pe.wait_ge(m_add, NB * t + w + 1)
                        pe.matmul(bank[0][:, 0:D + 1], onehot[:, 0, 0, :], ring[:, 0, 0:D + 1],
                                  start=True, stop=True).then_inc(m_sum, 1)
            def turn_block(n, s, staged, copied, turned):
                pe.wait_ge(staged[s], n + 1)
                pe.wait_ge(copied[s], n + 1)
                turn(bank[s], stage[s]).then_inc(turned[s], 1)

            def product(n, s, copied, used, weights, width, done):
                pe.wait_ge(copied[s], n + 2)
                pe.wait_ge(used[s], n + 1)
                for k in range(DK):
                    last = pe.matmul(bank[2 + s][:, 0:width], stage_t[s][:, k, :], weights[:, k, :],
                                     start=(k == 0), stop=(k == DK - 1))
                last.then_inc(done[s], 1)

            for turns, products in (((n_staged, n_copied, n_turned), (n_copied, x1_ready, wn_sb, D, n_product)),
                                    ((r_staged, r_copied, r_turned), (r_copied, logit_ready, wr_sb, NE, r_product))):
                turn_block(0, 0, *turns)
                with pe.Fori(0, NB // 2) as i:
                    turn_block(i, 1, *turns)
                    product(i, 0, *products)
                    turn_block(i + 1, 0, *turns)
                    product(i, 1, *products)
                product(NB // 2, 0, *products)
            pe.wait_ge(chosen, 3)
            pe.matmul(bank[6][:, 0:BE], upper[:, :], missed[:, 0:BE], start=True, stop=True).then_inc(counted, 1)
            pe.matmul(bank[7][:, 0:BE], ones[:, :], missed[:, 0:BE], start=True, stop=True).then_inc(counted, 1)
            pe.wait_ge(plan_ready, 1)
            pe.wait_ge(w1_in, 16 * (DK + 1))
            pe.wait_ge(w2_in, 16 * HK)
            pe.wait_ge(b2_in, 16)

            def expert_of(j):
                return pe.value_load(expert_i[0:1, bass.ds(j, 1)], min_val=0, max_val=NE - 1)

            def turn_rows(j, n, s):
                pe.wait_ge(row_in[s], 16 * (n + 1))
                if not isinstance(j, int) or j > 0:
                    pe.wait_ge(xt_ready, j)
                turn(bank[0], row[s]).then_inc(t_done, 1)

            def hidden(j, s):
                e = expert_of(j)
                pe.wait_ge(xt_ready, j + 1)
                if not isinstance(j, int) or j > 0:
                    pe.wait_ge(h_biased, j)
                for k in range(DK):
                    last = pe.matmul(bank[1][:, :], xt[s][:, k, :], w1_sb[:, k, bass.ds(e, 1), :], start=(k == 0), stop=(k == DK - 1))
                last.then_inc(h_done, 1)

            def turn_hidden(j):
                pe.wait_ge(gelu_done, j + 1)
                if not isinstance(j, int) or j > 0:
                    pe.wait_ge(ht_ready, j)
                for k in range(HK):
                    last = pe.transpose(bank[2][:, k * P:(k + 1) * P], hid[:, k * P:(k + 1) * P], ident[:, :])
                last.then_inc(gt_done, 1)

            def results(j):
                e = expert_of(j)
                pe.wait_ge(ht_ready, j + 1)
                if not isinstance(j, int) or j > 0:
                    pe.wait_ge(y_biased, j)
                for k in range(HK):
                    last = pe.matmul(bank[3][:, 0:D], ht[:, k, :], w2_sb[:, k, bass.ds(e, 1), :], start=(k == 0), stop=(k == HK - 1))
                last.then_inc(y_done, 1)

            def pe_step(j, n, s, peeled=False):
                turn_hidden(j - 1)
                s1 = (s + 1) % XS
                turn_rows(j + 1, n + (s + 1) // XS, s1)
                hidden(j, s)
                results(j - 1)

            turn_rows(0, 0, 0)
            turn_rows(1, 0, 1)
            hidden(0, 0)
            for j in (1, 2):
                pe_step(j, 0, j)
            with pe.Fori(1, NJ // XS - 1) as i:
                for s in range(XS):
                    pe_step(XS * i + s, i, s)
            for j in range(NJ - XS, NJ - 1):
                pe_step(j, j // XS, j % XS)
            turn_hidden(NJ - 2)
            hidden(NJ - 1, (NJ - 1) % XS)
            results(NJ - 2)
            turn_hidden(NJ - 1)
            results(NJ - 1)

        @block.vector
        def _(dve):
            for s in (*added, res_added, m_add, *x1_ready, *logit_ready, *r_copied):
                dve.sem_inc(s, 1)
            links = [0]

            def link(ins):
                links[0] += 1
                ins.then_inc(chain, 1)
                dve.wait_ge(chain, links[0])

            def scale_and_shift(lo, hi, n):
                dve.tensor_scalar(rstd[:, lo:hi], mv[:, lo:hi, 1], EPS, None, ALU.add).then_inc(var_ready, 1)
                dve.wait_ge(root_ready, n)
                link(dve.reciprocal(rstd[:, lo:hi], rstd[:, lo:hi]))
                return dve.scalar_tensor_tensor(out=nmr[:, lo:hi], in0=mv[:, lo:hi, 0], scalar=-1.0,
                                                in1=rstd[:, lo:hi], op0=ALU.mult, op1=ALU.mult)

            dve.wait_ge(dst_in, 16)
            dve.tensor_copy(base_f, dst_i[0:1, :].rearrange("p (g t) -> p g t", t=GT)[:, :, 0]).then_inc(base_ready, 1)
            for c in range(LC_N):
                dve.wait_ge(x_in[c], 16)
                for b in range(c * LC, (c + 1) * LC):
                    last = dve.bn_stats(stats[:, b, :], res[:, b, :])
                link(last)
                for b in range(c * LC, (c + 1) * LC):
                    last = dve.bn_aggr(mv[:, b, :], stats[:, b, :])
                link(last)
                scale_and_shift(c * LC, (c + 1) * LC, c + 1).then_inc(stats_ready, 1)
            dve.wait_ge(base_bc, 1)
            dve.wait_ge(consts, 7)
            link(dve.tensor_copy(base_i[:, :], bank[6][:, 0:NG]))
            by_group = inside[:, :].rearrange("p (g t) -> p g t", t=GT)
            link(dve.tensor_tensor(by_group, dst_i[:, :].rearrange("p (g t) -> p g t", t=GT),
                                   base_i[:, :].unsqueeze(2).broadcast_to([P, NG, GT]), ALU.subtract))
            link(dve.tensor_scalar(missed[:, :], inside[:, :], 0.0, None, ALU.is_ge))
            link(dve.tensor_scalar(target[:, :], inside[:, :], float(P), None, ALU.is_lt))
            link(dve.tensor_tensor(inside[:, :], missed[:, :], target[:, :], ALU.mult))
            link(dve.tensor_scalar(target[:, :], inside[:, :], -1.0, 1.0, ALU.mult, ALU.add))
            link(dve.tensor_reduce(n_missed[:, 0:1], target[:, :], AX.X, ALU.add))
            dve.sem_inc(miss_sum, 1)
            link(dve.scalar_tensor_tensor(out=missed[:, :], in0=dst_i[:, :], scalar=1.0, in1=target[:, :],
                                          op0=ALU.add, op1=ALU.mult))
            link(dve.tensor_scalar(missed[:, :], missed[:, :], -1.0, None, ALU.add))
            link(dve.tensor_scalar(dst_i[:, :], dst_i[:, :], P - 1, None, ALU.bitwise_and))
            link(dve.scalar_tensor_tensor(out=target[:, :], in0=dst_i[:, :], scalar=1.0, in1=inside[:, :],
                                          op0=ALU.add, op1=ALU.mult))
            link(dve.tensor_scalar(target[:, :], target[:, :], -1.0, None, ALU.add))
            link(dve.tensor_scalar(block_i[:, :], base_i[0:1, :], 7, None, ALU.arith_shift_right))
            link(dve.tensor_scalar(base_i[:, :], base_i[:, :], P - 1, None, ALU.bitwise_and))
            link(dve.tensor_scalar(in_second[:, :], base_i[:, :], iota_p[:, 0:1], None, ALU.is_gt))
            link(dve.tensor_scalar(in_first[:, :], in_second[:, :], -1.0, 1.0, ALU.mult, ALU.add))
            dve.wait_ge(miss_bc, 1)
            dve.tensor_copy(missed_i[:, :], bank[7][0:1, 0:1]).then_inc(miss_ready, 1)
            dve.wait_ge(agg_zero, 1)

            def one_hots(i, q):
                dve.wait_ge(summed[q], i + 1)
                dve.tensor_tensor(onehot[:, q, :, :], iota[:, :].unsqueeze(1).broadcast_to([P, GT, P]),
                                  target[:, bass.ds(i * GS * GT + q * GT, GT)].unsqueeze(2).broadcast_to([P, GT, P]),
                                  ALU.is_equal).then_inc(hot_ready, 1)

            def add_sums(i, q):
                g = i * GS + q
                blk = dve.value_load(block_i[0:1, bass.ds(g, 1)], min_val=0, max_val=NB - 1)
                dve.wait_ge(summed[q], i + 2)
                if q:
                    dve.wait_ge(added[q - 1], i + 2)
                else:
                    dve.wait_ge(added[GS - 1], i + 1)
                for n, mask in ((0, in_first), (1, in_second)):
                    a = agg[:, bass.ds(blk + n, 1), 0:D + 1].rearrange("p o d -> p (o d)")
                    last = dve.scalar_tensor_tensor(out=a, in0=bank[q][:, 0:D + 1], scalar=mask[:, bass.ds(g, 1)],
                                                    in1=a, op0=ALU.mult, op1=ALU.add)
                last.then_inc(added[q], 1)

            with dve.Fori(0, NI) as i:
                one_hots(i, 0)
                for q in range(GS):
                    if q + 1 < GS:
                        one_hots(i, q + 1)
                    add_sums(i, q)
                dve.wait_ge(f_product, i + 2)
                r = res[:, bass.ds(i, 1), :].rearrange("p o d -> p (o d)")
                dve.tensor_tensor(r, r, bank[5][:, 0:D], ALU.add).then_inc(res_added, 1)
            n_miss = dve.value_load(missed_i[0:1, 0:1], min_val=0, max_val=NT * P)
            dve.wait_ge(added[GS - 1], NI + 1)
            with dve.If(n_miss > 0):
                with dve.Fori(0, NT) as t:
                    with dve.Fori(0, NB) as w:
                        dve.wait_ge(m_sum, NB * t + w + 1)
                        dve.tensor_scalar(onehot[:, 0, 0, :], iota[:, :], missed[:, bass.ds(t, 1)], None,
                                          ALU.is_equal).then_inc(m_hot, 1)
                        dve.wait_ge(m_hot, NB * t + w + 1)
                        m = missed[:, bass.ds(t, 1)]
                        dve.tensor_scalar(m, m, float(-P), None, ALU.add)
                        dve.wait_ge(m_sum, NB * t + w + 2)
                        a = agg[:, bass.ds(w, 1), 0:D + 1].rearrange("p o d -> p (o d)")
                        dve.tensor_tensor(a, a, bank[0][:, 0:D + 1], ALU.add).then_inc(m_add, 1)
                        dve.wait_ge(m_add, NB * t + w + 2)
            link(dve.tensor_scalar(nmr[:, :], agg[:, 0:NB, D], 1.0, None, ALU.max))
            dve.reciprocal(rstd[:, :], nmr[:, :]).then_inc(deg_ready, 1)
            dve.wait_ge(res_added, NB + 1)

            def x1_block(b, n, s):
                dve.wait_ge(n_product[s], n + 2)
                r = res[:, bass.ds(b, 1), :].rearrange("p o d -> p (o d)")
                dve.tensor_tensor(r, r, bank[2 + s][:, 0:D], ALU.add).then_inc(x1_ready[s], 1)
                dve.wait_ge(x1_ready[s], n + 2)
                dve.bn_stats(stats[:, bass.ds(b, 1), :].rearrange("p o d -> p (o d)"), r).then_inc(st1_ready, 1)

            with dve.Fori(0, NB // 2) as i:
                x1_block(2 * i, i, 0)
                x1_block(2 * i + 1, i, 1)
            x1_block(NB - 1, NB // 2, 0)
            dve.wait_ge(st1_ready, NB)
            for b in range(NB):
                last = dve.bn_aggr(mv[:, b, :], stats[:, b, :])
            link(last)
            scale_and_shift(0, NB, LC_N + 1).then_inc(st1_ready, 1)
            with dve.Fori(0, NB) as b:
                dve.wait_ge(z_ready, b + 1)
                dve.bn_stats(stats[:, bass.ds(b, 1), :].rearrange("p o d -> p (o d)"),
                             agg[:, bass.ds(b, 1), 0:D].rearrange("p o d -> p (o d)")).then_inc(st2_ready, 1)
            dve.wait_ge(st2_ready, NB)
            for b in range(NB):
                last = dve.bn_aggr(mv[:, b, :], stats[:, b, :])
            link(last)
            scale_and_shift(0, NB, LC_N + 2).then_inc(st2_ready, 1)
            def turned(n, s):
                dve.wait_ge(r_turned[s], n + 2)
                dve.wait_ge(r_product[s], n + 1)
                for k in range(DK):
                    last = dve.tensor_scalar(stage_t[s][:, k, :], bank[s][:, k * P:(k + 1) * P], gb_sb[:, 0, k:k + 1],
                                             gb_sb[:, 1, k:k + 1], ALU.mult, ALU.add)
                last.then_inc(r_copied[s], 1)

            def logit_block(b, n, s):
                dve.wait_ge(r_product[s], n + 2)
                dve.tensor_tensor(inside[:, bass.ds(b * NE, NE)], bank[2 + s][:, 0:NE], br_sb[:, :],
                                  ALU.add).then_inc(logit_ready[s], 1)

            turned(0, 0)
            with dve.Fori(0, NB // 2) as i:
                turned(i, 1)
                logit_block(2 * i, i, 0)
                turned(i + 1, 0)
                logit_block(2 * i + 1, i, 1)
            logit_block(NB - 1, NB // 2, 0)
            dve.wait_ge(logit_ready[0], NB // 2 + 2)
            dve.wait_ge(logit_ready[1], NB // 2 + 1)

            def over_e(t):
                return t.unsqueeze(2).broadcast_to([P, NB, NE])

            iota_e = iota[:, 0:NE].unsqueeze(1).broadcast_to([P, NB, NE])

            def choose(values, top, choice):
                link(dve.tensor_reduce(top, values, AX.X, ALU.max))
                link(dve.tensor_tensor(choice, values, over_e(top), ALU.is_lt))
                link(dve.scalar_tensor_tensor(out=choice, in0=choice, scalar=float(NE), in1=iota_e, op0=ALU.mult, op1=ALU.add))
                link(dve.tensor_reduce(i1, choice, AX.X, ALU.min))
                link(dve.tensor_tensor(choice, iota_e, over_e(i1), ALU.is_equal))

            choose(logits, v1, choice1)
            link(dve.tensor_scalar(work, choice1, -1.0, 1.0, ALU.mult, ALU.add))
            link(dve.tensor_tensor(work, work, logits, ALU.mult))
            link(dve.scalar_tensor_tensor(out=work, in0=choice1, scalar=LOWEST, in1=work, op0=ALU.mult, op1=ALU.add))
            choose(work, v2[:, :], choice2)
            link(dve.tensor_tensor(both, choice1, choice2, ALU.add))
            dve.tensor_tensor(v2[:, :], v2[:, :], v1, ALU.subtract).then_inc(chosen, 1)
            dve.wait_ge(chosen, 2)
            dve.tensor_scalar(v1, p2[:, :], 1.0, None, ALU.add).then_inc(chosen, 1)
            dve.wait_ge(chosen, 3)
            link(dve.reciprocal(p1[:, :], v1))
            link(dve.tensor_tensor(p2[:, :], p2[:, :], p1[:, :], ALU.mult))
            dve.wait_ge(counted, 2)
            link(dve.tensor_copy(total, bank[7][:, 0:BE].rearrange("p (b e) -> p b e", e=NE)))
            ones_b = ones[:, 0:NB]
            for e in range(NE):
                last = dve.tensor_tensor_scan(incl[:, :, e], ones_b, total[:, :, e], 0.0, ALU.mult, ALU.add)
            link(last)
            link(dve.tensor_scalar(tiles_i[:, :], incl[:, NB - 1, :], float(P - 1), None, ALU.add))
            link(dve.tensor_scalar(tiles_i[:, :], tiles_i[:, :], 7, None, ALU.arith_shift_right))
            link(dve.tensor_copy(tiles_f[:, :], tiles_i[:, :]))
            link(dve.tensor_tensor_scan(tiles_c[:, :], ones[:, 0:NE], tiles_f[:, :], 0.0, ALU.mult, ALU.add))
            link(dve.tensor_tensor(offset[:, :], tiles_c[:, :], tiles_f[:, :], ALU.subtract))
            link(dve.tensor_tensor(work, incl[:, :, :], total, ALU.subtract))
            link(dve.tensor_tensor(work, work, bank[6][:, 0:BE].rearrange("p (b e) -> p b e", e=NE), ALU.add))
            link(dve.scalar_tensor_tensor(out=work, in0=offset[:, :].unsqueeze(1).broadcast_to([P, NB, NE]), scalar=float(P),
                                          in1=work, op0=ALU.mult, op1=ALU.add))
            for k, choice in ((0, choice1), (1, choice2)):
                link(dve.tensor_tensor(total, choice, work, ALU.mult))
                link(dve.tensor_reduce(slot_f[:, k, :], total, AX.X, ALU.add))
            link(dve.tensor_copy(slot_i[:, :, :], slot_f))
            link(dve.tensor_tensor(reach, iota_j[:, :].unsqueeze(2).broadcast_to([1, NJ, NE]),
                                   tiles_c[0:1, :].unsqueeze(1).broadcast_to([1, NJ, NE]), ALU.is_ge))
            link(dve.tensor_reduce(expert_f, reach, AX.X, ALU.add))
            link(dve.tensor_scalar(expert_i[:, :], expert_f, float(NE - 1), None, ALU.min))
            dve.wait_ge(xn_ready, NB)
            link(dve.tensor_copy(agg[:, 0:NB, D + 1], node_no[:, :]))
            dve.tensor_copy(agg[:, 0:NB, D], p1[:, :]).then_inc(plan_ready, 1)
            dve.wait_ge(scattered, 16 * NB)
            dve.tensor_copy(agg[:, 0:NB, D], p2[:, :]).then_inc(p2_set, 1)

            dve.wait_ge(w1_in, 16 * (DK + 1))
            dve.wait_ge(b2_in, 16)

            def expert_of(j):
                return dve.value_load(expert_i[0:1, bass.ds(j, 1)], min_val=0, max_val=NE - 1)

            def rows_turned(j, s):
                dve.wait_ge(t_done, j + 1)
                for k in range(DK):
                    last = dve.tensor_scalar(xt[s][:, k, :], bank[0][:, k * P:(k + 1) * P], gb_sb[:, 0, k:k + 1],
                                             gb_sb[:, 1, k:k + 1], ALU.mult, ALU.add)
                last.then_inc(xt_ready, 1)
                if not isinstance(j, int) or j >= XS:
                    dve.wait_ge(y_ready, j - XS + 1)
                dve.tensor_copy(row_tail[s][:, :], row[s][:, D:R]).then_inc(row_free, 1)

            def hidden_bias(j):
                e = expert_of(j)
                dve.wait_ge(h_done, j + 1)
                if not isinstance(j, int) or j > 0:
                    dve.wait_ge(gt_done, j)
                dve.tensor_tensor(hid, bank[1][:, :], b1_sb[:, bass.ds(e, 1), :].rearrange("p o h -> p (o h)"),
                                  ALU.add).then_inc(h_biased, 1)

            def weighted(j, s):
                e = expert_of(j)
                dve.wait_ge(y_done, j + 1)
                if not isinstance(j, int) or j >= XS:
                    dve.wait_ge(y_free, j - XS + 1)
                dve.tensor_copy(row_id[s][:, :], row_tail[s][:, 1:2])
                dve.tensor_tensor(y_out[s], bank[3][:, 0:D], b2_sb[:, bass.ds(e, 1), :].rearrange("p o d -> p (o d)"),
                                  ALU.add).then_inc(y_biased, 1)
                dve.wait_ge(y_biased, j + 1)
                dve.tensor_scalar(y_out[s], y_out[s], row_tail[s][:, 0:1], None, ALU.mult).then_inc(y_ready, 1)

            def dve_step(j, s):
                rows_turned(j + 1, (s + 1) % XS)
                hidden_bias(j)
                weighted(j - 1, (s - 1) % XS)

            rows_turned(0, 0)
            rows_turned(1, 1)
            hidden_bias(0)
            for j in range(1, XS + 1):
                dve_step(j, j % XS)
            for j in range(XS + 1, 2 * XS):
                dve_step(j, j % XS)
            with dve.Fori(2, NJ // XS - 1) as i:
                for s in range(XS):
                    dve_step(XS * i + s, s)
            for j in range(NJ - XS, NJ - 1):
                dve_step(j, j % XS)
            hidden_bias(NJ - 1)
            weighted(NJ - 2, (NJ - 2) % XS)
            weighted(NJ - 1, (NJ - 1) % XS)


def kernel(x, src, dst, L0_gnn_W_self, L0_gnn_W_neigh, L0_gnn_b, L0_ffn_gamma, L0_ffn_beta, L0_ffn_Wr, L0_ffn_br,
           L0_ffn_W1, L0_ffn_b1, L0_ffn_W2, L0_ffn_b2):
    import numpy as np
    import concourse.bacc as bacc
    from concourse.bass_utils import run_bass_kernel_spmd

    n, d = x.shape
    lc = LC * P
    n_pad = -(-n // lc) * lc
    e_pad = -(-len(src) // (P * GT * GS)) * (P * GT * GS)

    def columns(a, fill):
        whole = np.full(e_pad, fill, a.dtype)
        whole[:len(a)] = a
        return np.ascontiguousarray(whole.reshape(-1, P).T)

    x_pad = np.zeros((n_pad, d), x.dtype)
    x_pad[:n] = x
    arrays = {
        "x": x_pad, "src": columns(np.asarray(src), 0), "dst": columns(np.asarray(dst), n_pad - 1),
        "w_self": L0_gnn_W_self, "w_neigh": L0_gnn_W_neigh, "b_gnn": np.reshape(L0_gnn_b, (1, -1)),
        "gamma": np.reshape(L0_ffn_gamma, (-1, P)).T, "beta": np.reshape(L0_ffn_beta, (-1, P)).T,
        "w_r": L0_ffn_Wr, "b_r": np.reshape(L0_ffn_br, (1, -1)),
        "w1": L0_ffn_W1, "b1": np.reshape(L0_ffn_b1, (1, -1)), "w2": L0_ffn_W2, "b2": np.reshape(L0_ffn_b2, (1, -1)),
    }
    nc = bacc.Bacc("TRN2", target_bir_lowering=False, num_devices=1)
    feeds, args = {}, {}
    for name, a in arrays.items():
        a = np.ascontiguousarray(a)
        feeds[f"in_{name}"] = a
        args[name] = nc.dram_tensor(f"in_{name}", a.shape, mybir.dt.from_np(a.dtype), kind="ExternalInput").ap()
    out = nc.dram_tensor("out", (n_pad + P, d), F32, kind="ExternalOutput").ap()
    build(nc, out=out, **args)
    got = run_bass_kernel_spmd(nc, [feeds], core_ids=[0]).results[0]["out"]
    return got[:n]
```

```python
from contextlib import ExitStack

import concourse.bass as bass
from concourse import mybir

P = 128
F32 = mybir.dt.float32
I32 = mybir.dt.int32
ALU = mybir.AluOpType
ACT = mybir.ActivationFunctionType
AX = mybir.AxisListType
EPS = 1e-5

GT = 4
GS = 4
LC = 7
XS = 3
LM = 7
LOWEST = -3.0e38


def build(nc, x, src, dst, w_self, w_neigh, b_gnn, gamma, beta, w_r, b_r, w1, b1, w2, b2, out):
    NP, D = x.shape
    NB = NP // P
    NT = src.shape[1]
    NG = NT // GT
    NI = NG // GS
    DK = D // P
    NE, _, H = w1.shape
    HK = H // P
    R = D + 2
    NJ = (2 * NP + NE * (P - 1)) // P
    LC_N = NB // LC
    assert NB % LC == 0 and NG % GS == 0 and NI == NB and NJ % XS == 0 and NB * NE <= 512

    table = nc.dram_tensor("feature_table", [NP, D], F32, kind="Internal").ap()
    rows_tab = nc.dram_tensor("expert_rows", [NP + P, R], F32, kind="Internal").ap()

    def load_values(engine, row, most, **check):
        return nc.values_load_multi_w_load_instructions(row, engines=[engine], min_val=0, max_val=most, **check)[1]

    unchecked = {"skip_runtime_bounds_check_because": "worked out on the chip from node numbers, within these bounds"}

    with ExitStack() as ctx:
        def sb(name, shape, dt=F32):
            return ctx.enter_context(nc.sbuf_tensor(name, shape, dt))

        def sem(name):
            return ctx.enter_context(nc.semaphore(name))

        bank = [ctx.enter_context(nc.psum_tensor(f"bank{i}", [P, 512], F32)) for i in range(8)]

        res = sb("res", [P, NB, D])
        w2_sb = res[:, :, :].rearrange("p b d -> p (b d)")[:, 0:HK * NE * D].rearrange("p (k e d) -> p k e d", k=HK, e=NE)
        WF = max(NB * D, NE * DK * H + NE * H)
        feat_region = sb("feat_region", [P, WF])
        feat = feat_region[:, 0:NB * D].rearrange("p (b d) -> p b d", d=D)
        w1_sb = feat_region[:, 0:NE * DK * H].rearrange("p (k e h) -> p k e h", k=DK, e=NE)
        b1_sb = feat_region[:, NE * DK * H:NE * DK * H + NE * H].rearrange("p (e h) -> p e h", e=NE)
        agg = sb("agg", [P, NB + 1, R])
        ring = sb("ring", [P, GS * GT, R])
        pool_a = ring[:, :, :].rearrange("p a r -> p (a r)")
        onehot = sb("onehot", [P, GS, GT, P])
        onehot_flat = onehot[:, :, :, :].rearrange("p a b c -> p (a b c)")
        ws_sb = sb("ws_sb", [P, DK, D])
        wn_sb = sb("wn_sb", [P, DK, D])
        bg_sb = sb("bg_sb", [1, D])
        wr_sb = sb("wr_sb", [P, DK, NE])
        br_sb = sb("br_sb", [P, NE])
        gb_sb = sb("gb_sb", [P, 2, DK])
        ident = sb("ident", [P, P])
        upper = sb("upper", [P, P])
        ones = sb("ones", [P, P])
        zrow = sb("zrow", [P, 1, R])
        iota = sb("iota", [P, P])
        iota_p = sb("iota_p", [P, 1])
        node_no = sb("node_no", [P, NB])
        empty_no = sb("empty_no", [P, 1])
        src_sb = sb("src_sb", [P, NT + 3 * GT], I32)
        idx = sb("idx", [P, GS, GT], I32)
        dst_i = sb("dst_i", [P, NT], I32)
        inside = sb("inside", [P, NT])
        target_all = sb("target", [P, NT + 2 * GT])
        target = target_all[:, 0:NT]
        missed = sb("missed", [P, NT])
        base_i = sb("base_i", [P, NG], I32)
        block_i = sb("block_i", [1, NG], I32)
        in_first = sb("in_first", [P, NG])
        base_f = in_first[0:1, :]
        in_second = sb("in_second", [P, NG])
        n_missed = sb("n_missed", [P, 2])
        missed_i = sb("missed_i", [1, 1], I32)
        stats = sb("stats", [P, NB, 6])
        mv = sb("mv", [P, NB, 2])
        rstd = sb("rstd", [P, NB])
        nmr = sb("nmr", [P, NB])
        stage = sb("stage", [P, D])
        stage_f = sb("stage_f", [P, DK, P])
        experts = sb("experts", [1, NJ // XS, XS + 1], I32)

        BE = NB * NE
        assert 2 * BE <= NT

        def be(t, n):
            return t[:, n * BE:(n + 1) * BE].rearrange("p (b e) -> p b e", e=NE)

        edge_f = target
        logits, choice1 = be(inside, 0), be(inside, 1)
        choice2, work = be(target, 0), be(target, 1)
        both, total = be(missed, 0), be(missed, 1)
        incl = sb("incl", [P, NB, NE])
        incl_flat = incl[:, :, :].rearrange("p b e -> p (b e)")
        stats_flat = stats[:, :, :].rearrange("p b s -> p (b s)")
        dst_flat = dst_i[:, :].bitcast(F32)
        mean_rows = [dst_flat[:, c * D:(c + 1) * D] for c in range(2)]
        normal_rows = [missed[:, c * D:(c + 1) * D] for c in range(2)]
        mean_t = [a.rearrange("p (k t) -> p k t", k=DK) for a in (dst_flat[:, 2 * D:3 * D], incl_flat[:, 0:D])]
        normal_t = [a.rearrange("p (k t) -> p k t", k=DK) for a in (inside[:, BE:BE + D], stats_flat[:, 0:D])]
        nstats = [sb(f"nstats{c}", [P, 6]) for c in range(2)]
        nmv = [sb(f"nmv{c}", [P, 2]) for c in range(2)]
        nscale = [sb(f"nscale{c}", [P, 1]) for c in range(2)]
        nshift = [sb(f"nshift{c}", [P, 1]) for c in range(2)]
        ninv = [sb(f"ninv{c}", [P, 1]) for c in range(2)]
        rounds = sb("rounds", [1, NI + 1, 4], I32)
        upto = sb("upto", [1, NI + 1])
        fine = sb("fine", [1, 2])
        assert 3 * D <= NT and D <= BE and D <= 6 * NB
        v1 = stats_flat[:, 2 * NB:3 * NB]
        v2 = rstd
        i1 = stats_flat[:, 3 * NB:4 * NB]
        p1 = nmr
        p2 = sb("p2", [P, NB])
        slot_f = stats_flat[:, 0:2 * NB].rearrange("p (k b) -> p k b", k=2)
        slot_i = mv[:, :, :].rearrange("p b s -> p (b s)").bitcast(I32).rearrange("p (k b) -> p k b", k=2)
        part_i = base_i[:, 0:2 * NB].rearrange("p (k b) -> p k b", k=2)
        slot_row = stats_flat[:, 4 * NB:6 * NB]
        slot_tile = in_second[:, 0:2 * NB]
        signed_no = in_second[:, 2 * NB:4 * NB]
        tiles_i = sb("tiles_i", [P, NE], I32)
        tiles_f = sb("tiles_f", [P, NE])
        tiles_c = sb("tiles_c", [P, NE])
        offset = sb("offset", [P, NE])
        reach = onehot_flat[0:1, 0:NJ * NE].rearrange("p (j e) -> p j e", e=NE)
        expert_f = in_first[0:1, 0:NJ]

        hots = onehot_flat[:, 0:2 * LM * P].rearrange("p (s m c) -> p s m c", s=2, m=LM)
        picks = pool_a[:, NE * D:NE * D + 2 * LM * NJ].rearrange("p (s m j) -> p s m j", s=2, m=LM)
        of_slot = target[:, 0:NJ]
        is_empty = target[:, NJ:2 * NJ]
        of_choice = inside[:, 0:2 * NJ].rearrange("p (j k) -> p j k", k=2)
        node_i = base_i[:, 0:NJ]
        b2_sb = pool_a[:, 0:NE * D].rearrange("p (e d) -> p e d", e=NE)
        behind = res[:, :, :].rearrange("p b d -> p (b d)")[:, HK * NE * D:]
        row = [behind[:, s * R:(s + 1) * R] for s in range(XS)]
        y_out = [behind[:, XS * R + s * D:XS * R + (s + 1) * D] for s in range(XS)]
        xt = [behind[:, XS * (R + D) + s * D:XS * (R + D) + (s + 1) * D].rearrange("p (k t) -> p k t", k=DK) for s in range(XS)]
        weight = [sb(f"weight{s}", [P, 2]) for s in range(XS)]
        row_id = [sb(f"row_id{s}", [P, 1], I32) for s in range(XS)]
        add_id = [sb(f"add_id{s}", [P, 1], I32) for s in range(XS)]
        hid = pool_a[:, NE * D:NE * D + H]
        ht = pool_a[:, NE * D + H:NE * D + 2 * H].rearrange("p (k t) -> p k t", k=HK)
        assert NE * D + max(2 * H, 2 * LM * NJ) <= GS * GT * R and HK * NE * D + XS * (R + 2 * D) <= NB * D
        assert 2 * NJ <= NT and (2 * NB) % (2 * LM) == 0 and NJ <= P

        small_in = sem("small_in")
        dst_in = sem("dst_in")
        src_in = sem("src_in")
        x_in = [sem(f"x_in{c}") for c in range(LC_N)]
        w2_in = sem("w2_in")
        w1_in = sem("w1_in")
        b2_in = sem("b2_in")
        consts = sem("consts")
        zeroed = sem("zeroed")
        agg_zero = sem("agg_zero")
        ring_ones = sem("ring_ones")
        var_ready = sem("var_ready")
        root_ready = sem("root_ready")
        stats_ready = sem("stats_ready")
        feat_ready = sem("feat_ready")
        table_out = sem("table_out")
        base_ready = sem("base_ready")
        base_bc = sem("base_bc")
        miss_sum = sem("miss_sum")
        miss_bc = sem("miss_bc")
        miss_ready = sem("miss_ready")
        rounds_ready = sem("rounds_ready")
        idx_ready = sem("idx_ready")
        gathered = [sem(f"gathered{q}") for q in range(GS)]
        hot_ready = sem("hot_ready")
        summed = [sem(f"summed{q}") for q in range(GS)]
        added = [sem(f"added{q}") for q in range(GS)]
        f_staged = sem("f_staged")
        f_turned = sem("f_turned")
        f_copied = sem("f_copied")
        f_product = sem("f_product")
        res_added = sem("res_added")
        m_idx = sem("m_idx")
        m_gathered = sem("m_gathered")
        m_hot = sem("m_hot")
        m_sum = sem("m_sum")
        m_add = sem("m_add")
        edges_done = sem("edges_done")
        deg_max, deg_inv, mean_set, mean_turned, mean_copied, neigh_done = (sem(n) for n in (
            "deg_max", "deg_inv", "mean_set", "mean_turned", "mean_copied", "neigh_done"))
        x1_done, xn_done, row_done, xn_turned, xn_copied, router_done, logit_done = (sem(n) for n in (
            "x1_done", "xn_done", "row_done", "xn_turned", "xn_copied", "router_done", "logit_done"))
        ln = [{n: sem(f"ln{k}_{n}") for n in ("stats", "mv", "var", "root", "scale", "shift", "out")} for k in range(2)]
        x1_out = sem("x1_out")
        chosen = sem("chosen")
        counted = sem("counted")
        rows_done = sem("rows_done")
        rows_out = sem("rows_out")
        hots_ready = [sem(f"hots_ready{s}") for s in range(2)]
        picks_ready = [sem(f"picks_ready{s}") for s in range(2)]
        picked = [sem(f"picked{s}") for s in range(2)]
        lists_summed = sem("lists_summed")
        lists_ready = sem("lists_ready")
        id_set = sem("id_set")
        weight_set = sem("weight_set")
        row_in = [sem(f"row_in{s}") for s in range(XS)]
        row_free = sem("row_free")
        t_done = sem("t_done")
        xt_ready = sem("xt_ready")
        h_done = sem("h_done")
        h_biased = sem("h_biased")
        gelu_done = sem("gelu_done")
        gt_done = sem("gt_done")
        ht_ready = sem("ht_ready")
        y_done = sem("y_done")
        y_ready = sem("y_ready")
        y_free = sem("y_free")
        y_biased = sem("y_biased")
        y_added = sem("y_added")
        chain = sem("chain")
        gate = sem("gate")
        gate_pe = sem("gate_pe")
        gate_act = sem("gate_act")
        gate_dve = sem("gate_dve")

        block = ctx.enter_context(nc.Block())

        def rows(t):
            return t.rearrange("(b p) d -> p b d", p=P)

        x_v, table_v, out_v = rows(x), rows(table), rows(out[0:NP, :])
        rows_v = rows(rows_tab[0:NP, :])

        def round_work(engine, i):
            first, count, first_before, count_before = load_values(
                engine, rounds[0:1, bass.ds(i, 1), :].rearrange("p o n -> p (o n)"), NB - 2)
            return (first, count), (first_before, count_before), first + count

        def beside(engine, blocks, *steps):
            first, count = blocks
            with engine.If(count == 1):
                for step in steps:
                    step([(first, 0)])
            with engine.If(count > 1):
                for step in steps:
                    step([(first, 0), (first + 1, 1)])

        def rest(engine, begun, *steps):
            with engine.If(begun < NB - 2):
                with engine.Fori(0, NB - 2) as b:
                    with engine.If(b >= begun):
                        for step in steps:
                            step([(b, 0)])
            with engine.If(begun < NB - 1):
                for step in steps:
                    step([(NB - 2, 0), (NB - 1, 1)])
            with engine.If(begun == NB - 1):
                for step in steps:
                    step([(NB - 1, 0)])

        @block.sync
        def _(sp):
            sp.dma_start(dst_i[:, :], dst).then_inc(dst_in, 16)
            for c in range(LC_N):
                s = slice(c * LC, (c + 1) * LC)
                sp.dma_start(res[:, s, :], x_v[:, s, :]).then_inc(x_in[c], 16)
            sp.dma_start(src_sb[:, 0:NT], src).then_inc(src_in, 16)
            sp.dma_start(ws_sb[:, :, :], w_self.rearrange("(k p) n -> p k n", p=P)).then_inc(small_in, 16)
            sp.dma_start(wn_sb[:, :, :], w_neigh.rearrange("(k p) n -> p k n", p=P)).then_inc(small_in, 16)
            sp.dma_start(bg_sb[:, :], b_gnn).then_inc(small_in, 16)
            sp.dma_start(wr_sb[:, :, :], w_r.rearrange("(k p) n -> p k n", p=P)).then_inc(small_in, 16)
            sp.dma_start(br_sb[:, :], b_r.broadcast_to([P, NE])).then_inc(small_in, 16)
            sp.dma_start(gb_sb[:, 0, :], gamma).then_inc(small_in, 16)
            sp.dma_start(gb_sb[:, 1, :], beta).then_inc(small_in, 16)
            for c in range(LC_N):
                s = slice(c * LC, (c + 1) * LC)
                sp.wait_ge(feat_ready, (c + 1) * LC)
                sp.dma_start(table_v[:, s, :], feat[:, s, :]).then_inc(table_out, 16)
            sp.wait_ge(zeroed, 1)
            sp.dma_start(rows_tab[NP:NP + P, :], zrow[:, 0, :]).then_inc(rows_out, 16)
            sp.wait_ge(f_staged, NB)
            sp.wait_ge(table_out, 16 * LC_N)
            for k in range(DK):
                sp.dma_start(w1_sb[:, k, :, :], w1[:, k * P:(k + 1) * P, :].rearrange("e p h -> p e h")).then_inc(w1_in, 16)
            sp.dma_start(b1_sb, b1.broadcast_to([P, NE * H]).rearrange("p (e h) -> p e h", e=NE)).then_inc(w1_in, 16)
            sp.wait_ge(edges_done, 1)
            sp.dma_start(b2_sb, b2.broadcast_to([P, NE * D]).rearrange("p (e d) -> p e d", e=NE)).then_inc(b2_in, 16)
            sp.dma_start(out[NP:NP + P, :], zrow[:, 0, 0:D]).then_inc(x1_out, 16)
            sp.wait_ge(x1_done, NB)
            for c in range(LC_N):
                s = slice(c * LC, (c + 1) * LC)
                sp.dma_start(out_v[:, s, :], res[:, s, :]).then_inc(x1_out, 16)
            sp.wait_ge(ln[0]["out"], NB)
            sp.wait_ge(x1_out, 16 * (LC_N + 1))
            for k in range(HK):
                sp.dma_start(w2_sb[:, k, :, :], w2[:, k * P:(k + 1) * P, :].rearrange("e p d -> p e d")).then_inc(w2_in, 16)
            sp.wait_ge(rows_done, 1)
            for c in range(LC_N):
                s = slice(c * LC, (c + 1) * LC)
                sp.dma_start(rows_v[:, s, :], agg[:, s, :]).then_inc(rows_out, 16)
            sp.wait_ge(rows_out, 16 * (LC_N + 1))

        @block.gpsimd
        def _(pool):
            pool.memset(ones[:, :], 1.0).then_inc(consts, 1)
            pool.iota(iota[:, :], [[1, P]], base=0, channel_multiplier=0, allow_small_or_imprecise_dtypes=True).then_inc(consts, 1)
            pool.iota(iota_p[:, :], [[0, 1]], base=0, channel_multiplier=1, allow_small_or_imprecise_dtypes=True).then_inc(consts, 1)
            pool.iota(node_no[:, :], [[P, NB]], base=1, channel_multiplier=1, allow_small_or_imprecise_dtypes=True).then_inc(consts, 1)
            pool.iota(empty_no[:, :], [[0, 1]], base=NP + 1, channel_multiplier=1, allow_small_or_imprecise_dtypes=True).then_inc(consts, 1)
            pool.wait_ge(consts, 1)
            pool.affine_select(out=ident[:, :], in_=ones[:, :], compare_op=ALU.is_equal, fill=0.0,
                               base=0, pattern=[[-1, P]], channel_multiplier=1).then_inc(consts, 1)
            pool.affine_select(out=upper[:, :], in_=ones[:, :], compare_op=ALU.is_gt, fill=0.0,
                               base=0, pattern=[[1, P]], channel_multiplier=-1).then_inc(consts, 1)
            pool.memset(src_sb[:, NT:], 0).then_inc(consts, 1)
            pool.memset(zrow[:, :, :], 0.0).then_inc(zeroed, 1)
            pool.memset(ring[:, :, D:D + 1], 1.0).then_inc(ring_ones, 1)
            pool.memset(agg[:, :, :], 0.0).then_inc(agg_zero, 1)
            pool.wait_ge(table_out, 16 * LC_N)
            with pool.Fori(0, NI) as i:
                for q in range(GS):
                    pool.wait_ge(idx_ready, GS * i + q + 1)
                    pool.wait_ge(summed[q], i + 1)
                    pool.sem_inc(gate, 1)
                    for t in range(GT):
                        pool.indirect_dma_start(ring[:, q * GT + t, 0:D], None, table,
                                                bass.IndirectOffsetOnAxis(idx[:, q, t:t + 1], 0)).then_inc(gathered[q], 16)
            pool.wait_ge(miss_ready, 1)
            n_miss = pool.value_load(missed_i[0:1, 0:1], min_val=0, max_val=NT * P)
            for q in range(GS):
                pool.wait_ge(summed[q], NI + 1)
            with pool.If(n_miss > 0):
                with pool.Fori(0, NT) as t:
                    pool.wait_ge(m_sum, NB * t + 1)
                    pool.tensor_copy(idx[:, 0, 0:1], src_sb[:, bass.ds(t, 1)]).then_inc(m_idx, 1)
                    pool.wait_ge(m_idx, t + 1)
                    pool.sem_inc(gate, 1)
                    pool.indirect_dma_start(ring[:, 0, 0:D], None, table,
                                            bass.IndirectOffsetOnAxis(idx[:, 0, 0:1], 0)).then_inc(m_gathered, 16)

            with pool.Fori(0, NB // LM) as i:
                for s in range(2):
                    pool.wait_ge(hots_ready[s], i + 1)
                    pool.sem_inc(gate, 1)
                    pool.tensor_tensor(picks[:, s, :, :], picks[:, s, :, :],
                                       signed_no[:, bass.ds(2 * LM * i + LM * s, LM)].unsqueeze(2).broadcast_to([P, LM, NJ]),
                                       ALU.mult).then_inc(picks_ready[s], 1)

            def copy_id(to, j, n):
                pool.tensor_copy(to[:, :], node_i[:, bass.ds(j, 1)]).then_inc(id_set, 1)
                pool.wait_ge(id_set, n)
                pool.sem_inc(gate, 1)

            def gather_rows(j, s, n):
                copy_id(row_id[s], j, n)
                pool.indirect_dma_start(row[s], None, rows_tab, bass.IndirectOffsetOnAxis(row_id[s][:, :], 0)).then_inc(row_in[s], 16)

            def add_rows(j, s, n):
                copy_id(add_id[s], j, n)
                pool.wait_ge(y_ready, j + 1)
                pool.sem_inc(gate, 1)
                pool.indirect_dma_start(out, bass.IndirectOffsetOnAxis(add_id[s][:, :], 0),
                                        y_out[s], None, compute_op=ALU.add).then_inc(y_added, 16)

            def added_before(j):
                pool.wait_ge(y_added, 16 * j)
                pool.sem_inc(y_free, 1)

            def pool_step(j, s, first=False):
                if not first:
                    added_before(j)
                add_rows(j, s, 2 * j + XS + 2)
                pool.wait_ge(row_free, j + 2)
                gather_rows(j + XS + 1, (s + 1) % XS, 2 * j + XS + 3)

            pool.wait_ge(lists_ready, 1)
            pool.wait_ge(rows_out, 16 * (LC_N + 1))
            pool.wait_ge(x1_out, 16 * (LC_N + 1))
            for j in range(XS):
                gather_rows(j, j, j + 1)
            pool.wait_ge(row_free, 1)
            gather_rows(XS, 0, XS + 1)
            for j in range(XS):
                pool_step(j, j, first=(j == 0))
            with pool.Fori(1, NJ // XS - 2) as i:
                for s in range(XS):
                    pool_step(XS * i + s, s)
            for j in range(NJ - 2 * XS, NJ - XS - 1):
                pool_step(j, j % XS)
            for j in range(NJ - XS - 1, NJ):
                added_before(j)
                add_rows(j, j % XS, NJ + 1 + j)
            pool.wait_ge(y_added, 16 * NJ)

        @block.scalar
        def _(act):
            def root(lo, hi, n):
                act.wait_ge(var_ready, n)
                act.activation(rstd[:, lo:hi], rstd[:, lo:hi], ACT.Sqrt).then_inc(root_ready, 1)

            act.sem_inc(f_copied, 1)
            act.sem_inc(row_done, 1)
            act.sem_inc(mean_copied, 1)
            for c in range(LC_N):
                root(c * LC, (c + 1) * LC, c + 1)
                act.wait_ge(stats_ready, c + 1)
                for b in range(c * LC, (c + 1) * LC):
                    act.activation(feat[:, b, :], res[:, b, :], ACT.Identity, bias=nmr[:, b:b + 1],
                                   scale=rstd[:, b:b + 1]).then_inc(feat_ready, 1)
            act.wait_ge(feat_ready, NB)
            act.wait_ge(src_in, 16)

            def mean(blocks):
                for b, c in blocks:
                    act.wait_ge(deg_inv, b + 1)
                    act.sem_inc(gate_act, 1)
                    act.activation(mean_rows[c], agg[:, bass.ds(b, 1), 0:D], ACT.Copy, scale=ninv[c][:, 0:1]).then_inc(mean_set, 1)

            def mean_transposed(blocks):
                act.wait_ge(mean_turned, blocks[-1][0] + 1)
                for b, c in blocks:
                    act.copy(mean_t[c], bank[5][:, c * D:(c + 1) * D].rearrange("p (k t) -> p k t", k=DK)).then_inc(mean_copied, 1)

            def normal(k, blocks):
                if k == 1:
                    act.wait_ge(row_done, blocks[0][0] + 1)
                for b, c in blocks:
                    act.wait_ge(ln[k]["var"], b + 1)
                    act.activation(nscale[c][:, :], nscale[c][:, :], ACT.Sqrt).then_inc(ln[k]["root"], 1)
                for b, c in blocks:
                    act.wait_ge(ln[k]["shift"], b + 1)
                    act.sem_inc(gate_act, 1)
                    if k == 0:
                        act.activation(agg[:, bass.ds(b, 1), 0:D], res[:, bass.ds(b, 1), :], ACT.Identity,
                                       bias=nshift[c][:, 0:1], scale=nscale[c][:, 0:1]).then_inc(ln[0]["out"], 1)
                    else:
                        act.activation(normal_rows[c], agg[:, bass.ds(b, 1), 0:D], ACT.Identity, bias=nshift[c][:, 0:1],
                                       scale=nscale[c][:, 0:1]).then_inc(xn_done, 1)

            def normal_transposed(blocks):
                act.wait_ge(xn_turned, blocks[-1][0] + 1)
                for b, c in blocks:
                    for k in range(DK):
                        last = act.activation(normal_t[c][:, k, :], bank[7][:, c * D + k * P:c * D + (k + 1) * P], ACT.Identity,
                                              bias=gb_sb[:, 1, k:k + 1], scale=gb_sb[:, 0, k:k + 1])
                    last.then_inc(xn_copied, 1)
                for b, c in blocks:
                    act.activation(agg[:, bass.ds(b, 1), 0:D], normal_rows[c], ACT.Copy).then_inc(row_done, 1)

            def normal_0(blocks):
                normal(0, blocks)

            def normal_1(blocks):
                normal(1, blocks)

            def stage_idx(i, q):
                act.wait_ge(summed[q], i + 1)
                act.copy(idx[:, q, :], src_sb[:, bass.ds(i * GS * GT + q * GT, GT)]).then_inc(idx_ready, 1)

            act.wait_ge(consts, 8)
            stage_idx(0, 0)
            stage_idx(0, 1)
            stage_idx(0, 2)
            act.wait_ge(rounds_ready, 1)
            with act.Fori(0, NI) as i:
                now, before, begun = round_work(mybir.EngineType.Activation, i)
                for q in range(GS):
                    stage_idx(i + (q + 3) // GS, (q + 3) % GS)
                    if q == 0:
                        act.wait_ge(f_turned, i + 1)
                        act.copy(stage[:, :], feat[:, bass.ds(i, 1), :]).then_inc(f_staged, 1)
                        beside(act, now, mean)
                        beside(act, before, normal_1)
                    if q == 1:
                        beside(act, now, mean_transposed)
                    if q == 2:
                        act.wait_ge(f_turned, i + 2)
                        act.wait_ge(f_product, i + 1)
                        act.copy(stage_f[:, :, :], bank[4][:, 0:D].rearrange("p (k t) -> p k t", k=DK)).then_inc(f_copied, 1)
                        beside(act, before, normal_transposed)
                        beside(act, now, normal_0)
            now, before, begun = round_work(mybir.EngineType.Activation, NI)
            beside(act, before, normal_1, normal_transposed)
            rest(act, begun, mean, mean_transposed, normal_0, normal_1, normal_transposed)
            act.wait_ge(chosen, 1)
            act.activation(p2[:, :], v2[:, :], ACT.Exp).then_inc(chosen, 1)

            def gelu(j):
                act.wait_ge(h_biased, j + 1)
                act.activation(hid, hid, ACT.Gelu).then_inc(gelu_done, 1)

            def hidden_turned(j):
                act.wait_ge(gt_done, j + 1)
                if not isinstance(j, int) or j > 0:
                    act.wait_ge(y_done, j)
                act.copy(ht, bank[2][:, :].rearrange("p (k t) -> p k t", k=HK)).then_inc(ht_ready, 1)

            gelu(0)
            hidden_turned(0)
            with act.Fori(1, NJ) as j:
                gelu(j)
                hidden_turned(j)

        @block.tensor
        def _(pe):
            for s in (*picked, *summed, f_turned, f_product, m_sum, neigh_done):
                pe.sem_inc(s, 1)
            pe.wait_ge(consts, 7)
            pe.wait_ge(base_ready, 1)
            pe.matmul(bank[6][:, 0:NG], ones[0:1, :], base_f, start=True, stop=True).then_inc(base_bc, 1)
            pe.wait_ge(miss_sum, 1)
            pe.matmul(bank[7][0:1, 0:1], n_missed[:, 0:1], ones[:, 0:1], start=True, stop=True).then_inc(miss_bc, 1)
            pe.wait_ge(small_in, 16 * 7)
            pe.wait_ge(ring_ones, 1)

            def turn(to, block):
                for k in range(DK):
                    last = pe.transpose(to[:, k * P:(k + 1) * P], block[:, k * P:(k + 1) * P], ident[:, :])
                return last

            def product(to, turned, weights):
                for k in range(DK):
                    last = pe.matmul(to, turned[:, k, :], weights[:, k, :], start=(k == 0), stop=(k == DK - 1))
                return last

            def turn_mean(read, blocks):
                pe.wait_ge(logit_done, read + 1)
                for b, c in blocks:
                    pe.wait_ge(mean_set, b + 1)
                    turn(bank[5][:, c * D:(c + 1) * D], mean_rows[c]).then_inc(mean_turned, 1)

            def neighbours(blocks):
                for b, c in blocks:
                    pe.wait_ge(mean_copied, b + 2)
                    product(bank[6][:, c * D:(c + 1) * D], mean_t[c], wn_sb).then_inc(neigh_done, 1)

            def turn_normal(blocks):
                for b, c in blocks:
                    pe.wait_ge(xn_done, b + 1)
                    turn(bank[7][:, c * D:(c + 1) * D], normal_rows[c]).then_inc(xn_turned, 1)

            def router(begun, blocks):
                pe.wait_ge(mean_copied, begun + 1)
                for b, c in blocks:
                    pe.wait_ge(xn_copied, b + 1)
                    product(bank[5][:, c * NE:(c + 1) * NE], normal_t[c], wr_sb).then_inc(router_done, 1)

            pe.wait_ge(rounds_ready, 1)
            with pe.Fori(0, NI) as i:
                now, before, begun = round_work(mybir.EngineType.PE, i)
                for q in range(GS):
                    pe.wait_ge(hot_ready, GS * i + q + 1)
                    pe.wait_ge(gathered[q], 16 * GT * (i + 1))
                    pe.wait_ge(added[q], i + 1)
                    for t in range(GT):
                        last = pe.matmul(bank[q][:, 0:D + 1], onehot[:, q, t, :], ring[:, q * GT + t, 0:D + 1],
                                         start=(t == 0), stop=(t == GT - 1))
                    last.then_inc(summed[q], 1)
                    if q == 1:
                        pe.wait_ge(f_staged, i + 1)
                        pe.wait_ge(f_copied, i + 1)
                        pe.wait_ge(res_added, i + 1)
                        turn(bank[4], stage).then_inc(f_turned, 1)
                        beside(pe, now, lambda blocks: turn_mean(before[0], blocks))
                    if q == 2:
                        beside(pe, now, neighbours)
                        beside(pe, before, turn_normal)
                    if q == 3:
                        pe.wait_ge(f_copied, i + 2)
                        for k in range(DK):
                            pe.matmul(bank[4][:, D:2 * D], stage_f[:, k, :], ws_sb[:, k, :], start=(k == 0), stop=False)
                        pe.matmul(bank[4][:, D:2 * D], ones[0:1, :], bg_sb[:, :], start=False, stop=True).then_inc(f_product, 1)
                        beside(pe, before, lambda blocks: router(begun, blocks))
            pe.wait_ge(miss_ready, 1)
            n_miss = pe.value_load(missed_i[0:1, 0:1], min_val=0, max_val=NT * P)
            with pe.If(n_miss > 0):
                with pe.Fori(0, NT) as t:
                    pe.wait_ge(m_gathered, 16 * (t + 1))
                    pe.sem_inc(gate_pe, 1)
                    with pe.Fori(0, NB) as w:
                        pe.wait_ge(m_hot, NB * t + w + 1)
                        pe.wait_ge(m_add, NB * t + w + 1)
                        pe.matmul(bank[0][:, 0:D + 1], onehot[:, 0, 0, :], ring[:, 0, 0:D + 1],
                                  start=True, stop=True).then_inc(m_sum, 1)
            now, before, begun = round_work(mybir.EngineType.PE, NI)
            beside(pe, before, turn_normal, lambda blocks: router(begun, blocks))
            rest(pe, begun, lambda blocks: turn_mean(blocks[0][0], blocks), neighbours, turn_normal, lambda blocks: router(blocks[-1][0] + 1, blocks))
            pe.wait_ge(chosen, 3)
            pe.matmul(bank[6][:, 0:BE], upper[:, :], missed[:, 0:BE], start=True, stop=True).then_inc(counted, 1)
            pe.matmul(bank[7][:, 0:BE], ones[:, :], missed[:, 0:BE], start=True, stop=True).then_inc(counted, 1)
            def zeros_product(**flags):
                return pe.matmul(bank[4][:, 0:NJ], zrow[:, 0, 0:P], iota[:, 0:NJ], **flags)

            pe.wait_ge(zeroed, 1)
            zeros_product(start=True, stop=False)
            with pe.Fori(0, NB // LM) as i:
                for s in range(2):
                    pe.wait_ge(picks_ready[s], i + 1)
                    for m in range(LM):
                        last = pe.matmul(bank[4][:, 0:NJ], hots[:, s, m, :], picks[:, s, m, :], start=False, stop=False)
                    last.then_inc(picked[s], 1)
            zeros_product(start=False, stop=True).then_inc(lists_summed, 1)
            pe.wait_ge(w1_in, 16 * (DK + 1))
            pe.wait_ge(w2_in, 16 * HK)
            pe.wait_ge(b2_in, 16)

            def turn_rows(j, n, s):
                pe.wait_ge(row_in[s], 16 * (n + 1))
                if not isinstance(j, int) or j > 0:
                    pe.wait_ge(xt_ready, j)
                turn(bank[0], row[s]).then_inc(t_done, 1)

            def hidden(j, s, e):
                pe.wait_ge(xt_ready, j + 1)
                if not isinstance(j, int) or j > 0:
                    pe.wait_ge(h_biased, j)
                for k in range(DK):
                    last = pe.matmul(bank[1][:, :], xt[s][:, k, :], w1_sb[:, k, bass.ds(e, 1), :], start=(k == 0), stop=(k == DK - 1))
                last.then_inc(h_done, 1)

            def turn_hidden(j):
                pe.wait_ge(gelu_done, j + 1)
                if not isinstance(j, int) or j > 0:
                    pe.wait_ge(ht_ready, j)
                for k in range(HK):
                    last = pe.transpose(bank[2][:, k * P:(k + 1) * P], hid[:, k * P:(k + 1) * P], ident[:, :])
                last.then_inc(gt_done, 1)

            def results(j, e):
                pe.wait_ge(ht_ready, j + 1)
                if not isinstance(j, int) or j > 0:
                    pe.wait_ge(y_biased, j)
                for k in range(HK):
                    last = pe.matmul(bank[3][:, 0:D], ht[:, k, :], w2_sb[:, k, bass.ds(e, 1), :], start=(k == 0), stop=(k == HK - 1))
                last.then_inc(y_done, 1)

            def pe_step(j, n, s, e):
                turn_hidden(j - 1)
                turn_rows(j + 1, n + (s + 1) // XS, (s + 1) % XS)
                hidden(j, s, e[s + 1])
                results(j - 1, e[s])

            def pe_experts(i):
                return load_values(mybir.EngineType.PE, experts[0:1, bass.ds(i, 1), :].rearrange("p o s -> p (o s)"), NE - 1, **unchecked)

            e = pe_experts(0)
            turn_rows(0, 0, 0)
            turn_rows(1, 0, 1)
            hidden(0, 0, e[1])
            for j in range(1, XS):
                pe_step(j, 0, j, e)
            with pe.Fori(1, NJ // XS - 1) as i:
                e = pe_experts(i)
                for s in range(XS):
                    pe_step(XS * i + s, i, s, e)
            e = pe_experts(NJ // XS - 1)
            for j in range(NJ - XS, NJ - 1):
                pe_step(j, j // XS, j % XS, e)
            turn_hidden(NJ - 2)
            hidden(NJ - 1, XS - 1, e[XS])
            results(NJ - 2, e[XS - 1])
            turn_hidden(NJ - 1)
            results(NJ - 1, e[XS])

        @block.vector
        def _(dve):
            for s in (*added, res_added, m_add, logit_done):
                dve.sem_inc(s, 1)
            links = [0]

            def link(ins):
                links[0] += 1
                ins.then_inc(chain, 1)
                dve.wait_ge(chain, links[0])

            def scale_and_shift(lo, hi, n):
                dve.tensor_scalar(rstd[:, lo:hi], mv[:, lo:hi, 1], EPS, None, ALU.add).then_inc(var_ready, 1)
                dve.wait_ge(root_ready, n)
                link(dve.reciprocal(rstd[:, lo:hi], rstd[:, lo:hi]))
                return dve.scalar_tensor_tensor(out=nmr[:, lo:hi], in0=mv[:, lo:hi, 0], scalar=-1.0,
                                                in1=rstd[:, lo:hi], op0=ALU.mult, op1=ALU.mult)

            dve.wait_ge(dst_in, 16)
            dve.tensor_copy(base_f, dst_i[0:1, :].rearrange("p (g t) -> p g t", t=GT)[:, :, 0]).then_inc(base_ready, 1)
            for c in range(LC_N):
                dve.wait_ge(x_in[c], 16)
                for b in range(c * LC, (c + 1) * LC):
                    last = dve.bn_stats(stats[:, b, :], res[:, b, :])
                link(last)
                for b in range(c * LC, (c + 1) * LC):
                    last = dve.bn_aggr(mv[:, b, :], stats[:, b, :])
                link(last)
                scale_and_shift(c * LC, (c + 1) * LC, c + 1).then_inc(stats_ready, 1)
            dve.wait_ge(base_bc, 1)
            dve.wait_ge(consts, 7)
            link(dve.tensor_copy(base_i[:, :], bank[6][:, 0:NG]))
            by_group = inside[:, :].rearrange("p (g t) -> p g t", t=GT)
            link(dve.tensor_tensor(by_group, dst_i[:, :].rearrange("p (g t) -> p g t", t=GT),
                                   base_i[:, :].unsqueeze(2).broadcast_to([P, NG, GT]), ALU.subtract))
            link(dve.tensor_scalar(missed[:, :], inside[:, :], 0.0, None, ALU.is_ge))
            link(dve.tensor_scalar(target, inside[:, :], float(P), None, ALU.is_lt))
            link(dve.tensor_tensor(inside[:, :], missed[:, :], target, ALU.mult))
            link(dve.tensor_scalar(target, inside[:, :], -1.0, 1.0, ALU.mult, ALU.add))
            link(dve.tensor_reduce(n_missed[:, 0:1], target, AX.X, ALU.add))
            down = onehot_flat[0:1, 0:NG]
            link(dve.memset(down, 0.0))
            link(dve.tensor_tensor(down[:, 1:NG], base_i[0:1, 1:NG], base_i[0:1, 0:NG - 1], ALU.is_lt))
            link(dve.tensor_reduce(fine[:, 0:1], down, AX.X, ALU.add))
            dve.tensor_tensor(n_missed[0:1, 0:1], n_missed[0:1, 0:1], fine[:, 0:1], ALU.add).then_inc(miss_sum, 1)
            link(dve.scalar_tensor_tensor(out=missed[:, :], in0=dst_i[:, :], scalar=1.0, in1=target,
                                          op0=ALU.add, op1=ALU.mult))
            link(dve.tensor_scalar(missed[:, :], missed[:, :], -1.0, None, ALU.add))
            link(dve.tensor_scalar(dst_i[:, :], dst_i[:, :], P - 1, None, ALU.bitwise_and))
            link(dve.scalar_tensor_tensor(out=target, in0=dst_i[:, :], scalar=1.0, in1=inside[:, :],
                                          op0=ALU.add, op1=ALU.mult))
            link(dve.tensor_scalar(target, target, -1.0, None, ALU.add))
            link(dve.tensor_scalar(block_i[:, :], base_i[0:1, :], 7, None, ALU.arith_shift_right))
            link(dve.tensor_scalar(base_i[:, :], base_i[:, :], P - 1, None, ALU.bitwise_and))
            link(dve.tensor_scalar(in_second[:, :], base_i[:, :], iota_p[:, 0:1], None, ALU.is_gt))
            link(dve.tensor_scalar(in_first[:, :], in_second[:, :], -1.0, 1.0, ALU.mult, ALU.add))
            dve.wait_ge(miss_bc, 1)
            dve.tensor_copy(missed_i[:, :], bank[7][0:1, 0:1]).then_inc(miss_ready, 1)
            link(dve.tensor_scalar(fine[:, 1:2], bank[7][0:1, 0:1], 0.0, None, ALU.is_equal))
            link(dve.tensor_scalar(upto[:, 1:NI + 1], block_i[:, :].rearrange("p (i q) -> p i q", q=GS)[:, :, 0],
                                   fine[:, 1:2], None, ALU.mult))
            link(dve.tensor_tensor(upto[:, 1:NI + 1], upto[:, 1:NI + 1], iota[0:1, 0:NI], ALU.min))
            two = onehot_flat[0:1, 0:NI]
            link(dve.memset(two, 2.0))
            link(dve.memset(upto[:, 0:1], 0.0))
            link(dve.tensor_tensor_scan(upto[:, 1:NI + 1], two, upto[:, 1:NI + 1], 0.0, ALU.add, ALU.min))
            link(dve.memset(rounds[:, :, :], 0))
            dve.tensor_copy(rounds[:, :, 0], upto[:, :])
            dve.tensor_copy(rounds[:, 1:, 2], upto[:, 0:NI])
            dve.tensor_tensor(rounds[:, 0:NI, 1], upto[:, 1:NI + 1], upto[:, 0:NI], ALU.subtract)
            dve.tensor_tensor(rounds[:, 1:, 3], upto[:, 1:NI + 1], upto[:, 0:NI], ALU.subtract).then_inc(rounds_ready, 1)
            dve.wait_ge(agg_zero, 1)

            def one_hots(i, q):
                dve.wait_ge(summed[q], i + 1)
                dve.tensor_tensor(onehot[:, q, :, :], iota[:, :].unsqueeze(1).broadcast_to([P, GT, P]),
                                  target_all[:, bass.ds(i * GS * GT + q * GT, GT)].unsqueeze(2).broadcast_to([P, GT, P]),
                                  ALU.is_equal).then_inc(hot_ready, 1)

            def add_sums(i, q, blk):
                g = i * GS + q
                dve.wait_ge(summed[q], i + 2)
                if q:
                    dve.wait_ge(added[q - 1], i + 2)
                else:
                    dve.wait_ge(added[GS - 1], i + 1)
                for n, mask in ((0, in_first), (1, in_second)):
                    a = agg[:, bass.ds(blk + n, 1), 0:D + 1].rearrange("p o d -> p (o d)")
                    last = dve.scalar_tensor_tensor(out=a, in0=bank[q][:, 0:D + 1], scalar=mask[:, bass.ds(g, 1)],
                                                    in1=a, op0=ALU.mult, op1=ALU.add)
                last.then_inc(added[q], 1)

            dve.memset(target_all[:, NT:], -1.0).then_inc(chain, 1)
            links[0] += 1
            dve.wait_ge(chain, links[0])
            one_hots(0, 0)
            one_hots(0, 1)

            def degrees(blocks):
                for b, c in blocks:
                    dve.tensor_scalar(ninv[c][:, :], agg[:, bass.ds(b, 1), D], 1.0, None, ALU.max).then_inc(deg_max, 1)
                for b, c in blocks:
                    dve.wait_ge(deg_max, b + 1)
                    dve.reciprocal(ninv[c][:, :], ninv[c][:, :]).then_inc(deg_inv, 1)

            def moments(k, b, c, source):
                dve.bn_stats(nstats[c][:, :], source).then_inc(ln[k]["stats"], 1)
                dve.wait_ge(ln[k]["stats"], b + 1)
                dve.sem_inc(gate_dve, 1)
                dve.bn_aggr(nmv[c][:, :], nstats[c][:, :]).then_inc(ln[k]["mv"], 1)
                dve.wait_ge(ln[k]["mv"], b + 1)
                dve.tensor_scalar(nscale[c][:, :], nmv[c][:, 1:2], EPS, None, ALU.add).then_inc(ln[k]["var"], 1)

            def scales(k, blocks):
                for b, c in blocks:
                    dve.wait_ge(ln[k]["root"], b + 1)
                    dve.reciprocal(nscale[c][:, :], nscale[c][:, :]).then_inc(ln[k]["scale"], 1)
                for b, c in blocks:
                    dve.wait_ge(ln[k]["scale"], b + 1)
                    dve.scalar_tensor_tensor(out=nshift[c][:, :], in0=nmv[c][:, 0:1], scalar=-1.0, in1=nscale[c][:, :],
                                             op0=ALU.mult, op1=ALU.mult).then_inc(ln[k]["shift"], 1)

            def x1_sums(blocks):
                dve.wait_ge(neigh_done, blocks[-1][0] + 2)
                for b, c in blocks:
                    r = res[:, bass.ds(b, 1), :].rearrange("p o d -> p (o d)")
                    dve.tensor_tensor(r, r, bank[6][:, c * D:(c + 1) * D], ALU.add).then_inc(x1_done, 1)
                for b, c in blocks:
                    dve.wait_ge(x1_done, b + 1)
                    dve.sem_inc(gate_dve, 1)
                    moments(0, b, c, res[:, bass.ds(b, 1), :].rearrange("p o d -> p (o d)"))
                scales(0, blocks)

            def second_moments(blocks):
                for b, c in blocks:
                    dve.wait_ge(ln[0]["out"], b + 1)
                    dve.sem_inc(gate_dve, 1)
                    moments(1, b, c, agg[:, bass.ds(b, 1), 0:D].rearrange("p o d -> p (o d)"))
                scales(1, blocks)

            def add_router_bias(blocks):
                dve.wait_ge(router_done, blocks[-1][0] + 1)
                for b, c in blocks:
                    dve.tensor_tensor(inside[:, bass.ds(b * NE, NE)], bank[5][:, c * NE:(c + 1) * NE], br_sb[:, :],
                                      ALU.add).then_inc(logit_done, 1)

            with dve.Fori(0, NI) as i:
                blocks = load_values(mybir.EngineType.DVE, block_i[0:1, bass.ds(i * GS, GS)], NB - 1, **unchecked)
                now, before, begun = round_work(mybir.EngineType.DVE, i)
                for q in range(GS):
                    one_hots(i + (q + 2) // GS, (q + 2) % GS)
                    add_sums(i, q, blocks[q])
                    if q == 0:
                        beside(dve, now, degrees)
                        beside(dve, before, second_moments)
                    if q == 2:
                        beside(dve, now, x1_sums)
                    if q == 3:
                        beside(dve, before, add_router_bias)
                dve.wait_ge(f_product, i + 2)
                r = res[:, bass.ds(i, 1), :].rearrange("p o d -> p (o d)")
                dve.tensor_tensor(r, r, bank[4][:, D:2 * D], ALU.add).then_inc(res_added, 1)
            n_miss = dve.value_load(missed_i[0:1, 0:1], min_val=0, max_val=NT * P)
            dve.wait_ge(added[GS - 1], NI + 1)
            with dve.If(n_miss > 0):
                with dve.Fori(0, NT) as t:
                    with dve.Fori(0, NB) as w:
                        dve.wait_ge(m_sum, NB * t + w + 1)
                        dve.tensor_scalar(onehot[:, 0, 0, :], iota[:, :], missed[:, bass.ds(t, 1)], None,
                                          ALU.is_equal).then_inc(m_hot, 1)
                        dve.wait_ge(m_hot, NB * t + w + 1)
                        m = missed[:, bass.ds(t, 1)]
                        dve.tensor_scalar(m, m, float(-P), None, ALU.add)
                        dve.wait_ge(m_sum, NB * t + w + 2)
                        a = agg[:, bass.ds(w, 1), 0:D + 1].rearrange("p o d -> p (o d)")
                        dve.tensor_tensor(a, a, bank[0][:, 0:D + 1], ALU.add).then_inc(m_add, 1)
                        dve.wait_ge(m_add, NB * t + w + 2)
            dve.sem_inc(edges_done, 1)
            dve.wait_ge(res_added, NB + 1)
            now, before, begun = round_work(mybir.EngineType.DVE, NI)
            beside(dve, before, second_moments, add_router_bias)
            rest(dve, begun, degrees, x1_sums, second_moments, add_router_bias)
            dve.wait_ge(logit_done, NB + 1)

            def over_e(t):
                return t.unsqueeze(2).broadcast_to([P, NB, NE])

            iota_e = iota[:, 0:NE].unsqueeze(1).broadcast_to([P, NB, NE])

            def choose(values, top, choice):
                link(dve.tensor_reduce(top, values, AX.X, ALU.max))
                link(dve.tensor_tensor(choice, values, over_e(top), ALU.is_lt))
                link(dve.scalar_tensor_tensor(out=choice, in0=choice, scalar=float(NE), in1=iota_e, op0=ALU.mult, op1=ALU.add))
                link(dve.tensor_reduce(i1, choice, AX.X, ALU.min))
                link(dve.tensor_tensor(choice, iota_e, over_e(i1), ALU.is_equal))

            choose(logits, v1, choice1)
            link(dve.tensor_scalar(work, choice1, -1.0, 1.0, ALU.mult, ALU.add))
            link(dve.tensor_tensor(work, work, logits, ALU.mult))
            link(dve.scalar_tensor_tensor(out=work, in0=choice1, scalar=LOWEST, in1=work, op0=ALU.mult, op1=ALU.add))
            choose(work, v2[:, :], choice2)
            dve.wait_ge(row_done, NB + 1)
            link(dve.tensor_tensor(both, choice1, choice2, ALU.add))
            dve.tensor_tensor(v2[:, :], v2[:, :], v1, ALU.subtract).then_inc(chosen, 1)
            dve.wait_ge(chosen, 2)
            dve.tensor_scalar(v1, p2[:, :], 1.0, None, ALU.add).then_inc(chosen, 1)
            dve.wait_ge(chosen, 3)
            link(dve.reciprocal(p1[:, :], v1))
            link(dve.tensor_tensor(p2[:, :], p2[:, :], p1[:, :], ALU.mult))
            dve.tensor_copy(agg[:, 0:NB, D], p1[:, :])
            dve.tensor_copy(agg[:, 0:NB, D + 1], p2[:, :]).then_inc(rows_done, 1)
            dve.wait_ge(counted, 2)
            link(dve.tensor_copy(total, bank[7][:, 0:BE].rearrange("p (b e) -> p b e", e=NE)))
            ones_b = ones[:, 0:NB]
            for e in range(NE):
                last = dve.tensor_tensor_scan(incl[:, :, e], ones_b, total[:, :, e], 0.0, ALU.mult, ALU.add)
            link(last)
            link(dve.tensor_scalar(tiles_i[:, :], incl[:, NB - 1, :], float(P - 1), None, ALU.add))
            link(dve.tensor_scalar(tiles_i[:, :], tiles_i[:, :], 7, None, ALU.arith_shift_right))
            link(dve.tensor_copy(tiles_f[:, :], tiles_i[:, :]))
            link(dve.tensor_tensor_scan(tiles_c[:, :], ones[:, 0:NE], tiles_f[:, :], 0.0, ALU.mult, ALU.add))
            link(dve.tensor_tensor(offset[:, :], tiles_c[:, :], tiles_f[:, :], ALU.subtract))
            link(dve.tensor_tensor(work, incl[:, :, :], total, ALU.subtract))
            link(dve.tensor_tensor(work, work, bank[6][:, 0:BE].rearrange("p (b e) -> p b e", e=NE), ALU.add))
            link(dve.scalar_tensor_tensor(out=work, in0=offset[:, :].unsqueeze(1).broadcast_to([P, NB, NE]), scalar=float(P),
                                          in1=work, op0=ALU.mult, op1=ALU.add))
            for k, choice in ((0, choice1), (1, choice2)):
                link(dve.tensor_tensor(total, choice, work, ALU.mult))
                link(dve.tensor_reduce(slot_f[:, k, :], total, AX.X, ALU.add))
            link(dve.tensor_copy(slot_i[:, :, :], slot_f))
            link(dve.tensor_tensor(reach, iota[0:1, 0:NJ].unsqueeze(2).broadcast_to([1, NJ, NE]),
                                   tiles_c[0:1, :].unsqueeze(1).broadcast_to([1, NJ, NE]), ALU.is_ge))
            link(dve.tensor_reduce(expert_f, reach, AX.X, ALU.add))
            per_round = expert_f.rearrange("p (i s) -> p i s", s=XS)
            link(dve.memset(experts[:, 0, :], 0))
            dve.tensor_scalar(experts[:, :, 1:XS + 1], per_round, float(NE - 1), None, ALU.min)
            link(dve.tensor_scalar(experts[:, 1:, 0], per_round[:, 0:NJ // XS - 1, XS - 1], float(NE - 1), None, ALU.min))
            link(dve.tensor_scalar(part_i[:, :, :], slot_i[:, :, :], P - 1, None, ALU.bitwise_and))
            link(dve.tensor_copy(slot_row, part_i[:, :, :].rearrange("p k b -> p (k b)")))
            link(dve.tensor_scalar(slot_i[:, :, :], slot_i[:, :, :], 7, None, ALU.arith_shift_right))
            link(dve.tensor_copy(slot_tile, slot_i[:, :, :].rearrange("p k b -> p (k b)")))
            dve.tensor_copy(signed_no[:, 0:NB], node_no[:, :])
            link(dve.tensor_scalar(signed_no[:, NB:2 * NB], node_no[:, :], -1.0, None, ALU.mult))

            def pick(i, s):
                m0 = 2 * LM * i + LM * s
                dve.wait_ge(picked[s], i + 1)
                dve.tensor_tensor(hots[:, s, :, :], iota[:, :].unsqueeze(1).broadcast_to([P, LM, P]),
                                  slot_row[:, bass.ds(m0, LM)].unsqueeze(2).broadcast_to([P, LM, P]), ALU.is_equal)
                dve.tensor_tensor(picks[:, s, :, :], iota[:, 0:NJ].unsqueeze(1).broadcast_to([P, LM, NJ]),
                                  slot_tile[:, bass.ds(m0, LM)].unsqueeze(2).broadcast_to([P, LM, NJ]),
                                  ALU.is_equal).then_inc(hots_ready[s], 1)

            with dve.Fori(0, NB // LM) as i:
                for s in range(2):
                    pick(i, s)
            dve.wait_ge(lists_summed, 1)
            link(dve.tensor_scalar(of_choice[:, :, 1], bank[4][:, 0:NJ], 0.0, None, ALU.is_lt))
            link(dve.tensor_scalar(of_choice[:, :, 0], of_choice[:, :, 1], -1.0, 1.0, ALU.mult, ALU.add))
            link(dve.tensor_copy(is_empty, bank[4][:, 0:NJ]))
            link(dve.scalar_tensor_tensor(out=of_slot, in0=is_empty, scalar=-1.0, in1=is_empty, op0=ALU.mult, op1=ALU.max))
            link(dve.tensor_scalar(is_empty, of_slot, 0.0, None, ALU.is_equal))
            link(dve.scalar_tensor_tensor(out=of_slot, in0=is_empty, scalar=empty_no[:, 0:1], in1=of_slot, op0=ALU.mult, op1=ALU.add))
            dve.tensor_scalar(node_i, of_slot, -1.0, None, ALU.add).then_inc(lists_ready, 1)

            dve.wait_ge(w1_in, 16 * (DK + 1))
            dve.wait_ge(b2_in, 16)

            def rows_turned(j, s):
                dve.wait_ge(t_done, j + 1)
                for k in range(DK):
                    last = dve.tensor_scalar(xt[s][:, k, :], bank[0][:, k * P:(k + 1) * P], gb_sb[:, 0, k:k + 1],
                                             gb_sb[:, 1, k:k + 1], ALU.mult, ALU.add)
                last.then_inc(xt_ready, 1)
                if not isinstance(j, int) or j >= XS:
                    dve.wait_ge(y_ready, j - XS + 1)
                dve.tensor_tensor(weight[s][:, :], row[s][:, D:R],
                                  of_choice[:, bass.ds(j, 1), :].rearrange("p o k -> p (o k)"), ALU.mult).then_inc(row_free, 1)

            def hidden_bias(j, e):
                dve.wait_ge(h_done, j + 1)
                if not isinstance(j, int) or j > 0:
                    dve.wait_ge(gt_done, j)
                dve.tensor_tensor(hid, bank[1][:, :], b1_sb[:, bass.ds(e, 1), :].rearrange("p o h -> p (o h)"),
                                  ALU.add).then_inc(h_biased, 1)

            def weighted(j, s, e):
                dve.wait_ge(row_free, j + 1)
                dve.tensor_tensor(weight[s][:, 0:1], weight[s][:, 0:1], weight[s][:, 1:2], ALU.add).then_inc(weight_set, 1)
                dve.wait_ge(y_done, j + 1)
                if not isinstance(j, int) or j >= XS:
                    dve.wait_ge(y_free, j - XS + 1)
                dve.tensor_tensor(y_out[s], bank[3][:, 0:D], b2_sb[:, bass.ds(e, 1), :].rearrange("p o d -> p (o d)"),
                                  ALU.add).then_inc(y_biased, 1)
                dve.wait_ge(y_biased, j + 1)
                dve.wait_ge(weight_set, j + 1)
                dve.tensor_scalar(y_out[s], y_out[s], weight[s][:, 0:1], None, ALU.mult).then_inc(y_ready, 1)

            def dve_step(j, s, e):
                rows_turned(j + 1, (s + 1) % XS)
                hidden_bias(j, e[s + 1])
                weighted(j - 1, (s - 1) % XS, e[s])

            def dve_experts(i):
                return load_values(mybir.EngineType.DVE, experts[0:1, bass.ds(i, 1), :].rearrange("p o s -> p (o s)"), NE - 1, **unchecked)

            e = dve_experts(0)
            rows_turned(0, 0)
            rows_turned(1, 1)
            hidden_bias(0, e[1])
            for j in range(1, XS):
                dve_step(j, j, e)
            e = dve_experts(1)
            for j in range(XS, 2 * XS):
                dve_step(j, j % XS, e)
            with dve.Fori(2, NJ // XS - 1) as i:
                rows_turned(XS * i + 1, 1)
                e = dve_experts(i)
                for s in range(XS):
                    if s:
                        rows_turned(XS * i + s + 1, (s + 1) % XS)
                    hidden_bias(XS * i + s, e[s + 1])
                    weighted(XS * i + s - 1, (s - 1) % XS, e[s])
            e = dve_experts(NJ // XS - 1)
            for j in range(NJ - XS, NJ - 1):
                dve_step(j, j % XS, e)
            hidden_bias(NJ - 1, e[XS])
            weighted(NJ - 2, (NJ - 2) % XS, e[XS - 1])
            weighted(NJ - 1, (NJ - 1) % XS, e[XS])


def kernel(x, src, dst, L0_gnn_W_self, L0_gnn_W_neigh, L0_gnn_b, L0_ffn_gamma, L0_ffn_beta, L0_ffn_Wr, L0_ffn_br,
           L0_ffn_W1, L0_ffn_b1, L0_ffn_W2, L0_ffn_b2):
    import numpy as np
    import concourse.bacc as bacc
    from concourse.bass_utils import run_bass_kernel_spmd

    n, d = x.shape
    lc = LC * P
    n_pad = -(-n // lc) * lc
    e_pad = -(-len(src) // (P * GT * GS)) * (P * GT * GS)

    def columns(a, fill):
        whole = np.full(e_pad, fill, a.dtype)
        whole[:len(a)] = a
        return np.ascontiguousarray(whole.reshape(-1, P).T)

    x_pad = np.zeros((n_pad, d), x.dtype)
    x_pad[:n] = x
    arrays = {
        "x": x_pad, "src": columns(np.asarray(src), 0), "dst": columns(np.asarray(dst), n_pad - 1),
        "w_self": L0_gnn_W_self, "w_neigh": L0_gnn_W_neigh, "b_gnn": np.reshape(L0_gnn_b, (1, -1)),
        "gamma": np.reshape(L0_ffn_gamma, (-1, P)).T, "beta": np.reshape(L0_ffn_beta, (-1, P)).T,
        "w_r": L0_ffn_Wr, "b_r": np.reshape(L0_ffn_br, (1, -1)),
        "w1": L0_ffn_W1, "b1": np.reshape(L0_ffn_b1, (1, -1)), "w2": L0_ffn_W2, "b2": np.reshape(L0_ffn_b2, (1, -1)),
    }
    nc = bacc.Bacc("TRN2", target_bir_lowering=False, num_devices=1)
    feeds, args = {}, {}
    for name, a in arrays.items():
        a = np.ascontiguousarray(a)
        feeds[f"in_{name}"] = a
        args[name] = nc.dram_tensor(f"in_{name}", a.shape, mybir.dt.from_np(a.dtype), kind="ExternalInput").ap()
    out = nc.dram_tensor("out", (n_pad + P, d), F32, kind="ExternalOutput").ap()
    build(nc, out=out, **args)
    got = run_bass_kernel_spmd(nc, [feeds], core_ids=[0]).results[0]["out"]
    return got[:n]
```

```python
from contextlib import ExitStack

import concourse.bass as bass
from concourse import mybir

P = 128
F32 = mybir.dt.float32
I32 = mybir.dt.int32
ALU = mybir.AluOpType
ACT = mybir.ActivationFunctionType
AX = mybir.AxisListType
EPS = 1e-5

GT = 4
GS = 4
LC = 7
XS = 3
LM = 7
LS = 4
LOWEST = -3.0e38


def build(nc, x, src, dst, w_self, w_neigh, b_gnn, gamma, beta, w_r, b_r, w1, b1, w2, b2, out):
    NP, D = x.shape
    NB = NP // P
    NT = src.shape[1]
    NG = NT // GT
    NI = NG // GS
    DK = D // P
    NE, _, H = w1.shape
    HK = H // P
    R = D + 2
    NJ = (2 * NP + NE * (P - 1)) // P
    LC_N = NB // LC
    assert NB % LC == 0 and NG % GS == 0 and NI == NB and NJ % XS == 0 and NB * NE <= 512

    table = nc.dram_tensor("feature_table", [NP, D], F32, kind="Internal").ap()
    rows_tab = nc.dram_tensor("expert_rows", [NP + P, R], F32, kind="Internal").ap()

    def load_values(engine, row, most, **check):
        return nc.values_load_multi_w_load_instructions(row, engines=[engine], min_val=0, max_val=most, **check)[1]

    unchecked = {"skip_runtime_bounds_check_because": "worked out on the chip from node numbers, within these bounds"}

    with ExitStack() as ctx:
        def sb(name, shape, dt=F32):
            return ctx.enter_context(nc.sbuf_tensor(name, shape, dt))

        def sem(name):
            return ctx.enter_context(nc.semaphore(name))

        bank = [ctx.enter_context(nc.psum_tensor(f"bank{i}", [P, 512], F32)) for i in range(8)]

        res = sb("res", [P, NB, D])
        w2_sb = res[:, :, :].rearrange("p b d -> p (b d)")[:, 0:HK * NE * D].rearrange("p (k e d) -> p k e d", k=HK, e=NE)
        feat = sb("feat", [P, NB, D])
        feat_flat = feat[:, :, :].rearrange("p b d -> p (b d)")
        w1_sb = feat_flat[:, 0:NE * DK * H].rearrange("p (k e h) -> p k e h", k=DK, e=NE)
        w1_of = [feat_flat[:, (NE + s) * DK * H:(NE + s + 1) * DK * H].rearrange("p (k h) -> p k h", k=DK) for s in range(XS)]
        assert (NE + XS) * DK * H <= NB * D
        b1_sb = sb("b1_sb", [P, NE, HK])
        agg = sb("agg", [P, NB + 1, R])
        ring = sb("ring", [P, GS * GT, R])
        pool_a = ring[:, :, :].rearrange("p a r -> p (a r)")
        onehot = sb("onehot", [P, GS, GT, P])
        onehot_flat = onehot[:, :, :, :].rearrange("p a b c -> p (a b c)")
        ws_sb = sb("ws_sb", [P, DK, D])
        wn_sb = sb("wn_sb", [P, DK, D])
        bg_sb = sb("bg_sb", [1, D])
        wr_sb = sb("wr_sb", [P, DK, NE])
        br_sb = sb("br_sb", [P, NE])
        gb_sb = sb("gb_sb", [P, 2, DK])
        ident = sb("ident", [P, P])
        upper = sb("upper", [P, P])
        ones = sb("ones", [P, P])
        zrow = sb("zrow", [P, 1, R])
        iota = sb("iota", [P, P])
        iota_p = sb("iota_p", [P, 1])
        node_no = sb("node_no", [P, NB])
        empty_no = sb("empty_no", [P, 1])
        src_sb = sb("src_sb", [P, NT + 3 * GT], I32)
        idx = sb("idx", [P, GS, GT], I32)
        dst_i = sb("dst_i", [P, NT], I32)
        inside = sb("inside", [P, NT])
        target_all = sb("target", [P, NT + 2 * GT])
        target = target_all[:, 0:NT]
        missed = sb("missed", [P, NT])
        base_i = sb("base_i", [P, NG], I32)
        block_i = sb("block_i", [1, NG], I32)
        in_first = sb("in_first", [P, NG])
        base_f = in_first[0:1, :]
        in_second = sb("in_second", [P, NG])
        n_missed = sb("n_missed", [P, 2])
        missed_i = sb("missed_i", [1, 1], I32)
        stats = sb("stats", [P, NB, 6])
        mv = sb("mv", [P, NB, 2])
        rstd = sb("rstd", [P, NB])
        nmr = sb("nmr", [P, NB])
        stage = sb("stage", [P, D])
        stage_f = sb("stage_f", [P, DK, P])
        experts = sb("experts", [1, NJ // XS, XS + 1], I32)

        BE = NB * NE
        assert 2 * BE <= NT

        def be(t, n):
            return t[:, n * BE:(n + 1) * BE].rearrange("p (b e) -> p b e", e=NE)

        logits, choice1 = be(inside, 0), be(inside, 1)
        choice2, work = be(target, 0), be(target, 1)
        both, total = be(missed, 0), be(missed, 1)
        incl = sb("incl", [P, NB, NE])
        incl_flat = incl[:, :, :].rearrange("p b e -> p (b e)")
        stats_flat = stats[:, :, :].rearrange("p b s -> p (b s)")
        dst_flat = dst_i[:, :].bitcast(F32)
        mean_rows = [dst_flat[:, c * D:(c + 1) * D] for c in range(2)]
        normal_rows = [missed[:, c * D:(c + 1) * D] for c in range(2)]
        mean_t = [a.rearrange("p (k t) -> p k t", k=DK) for a in (dst_flat[:, 2 * D:3 * D], incl_flat[:, 0:D])]
        normal_t = [a.rearrange("p (k t) -> p k t", k=DK) for a in (inside[:, BE:BE + D], stats_flat[:, 0:D])]
        nstats = [sb(f"nstats{c}", [P, 6]) for c in range(2)]
        nmv = [sb(f"nmv{c}", [P, 2]) for c in range(2)]
        nscale = [sb(f"nscale{c}", [P, 1]) for c in range(2)]
        nshift = [sb(f"nshift{c}", [P, 1]) for c in range(2)]
        ninv = [sb(f"ninv{c}", [P, 1]) for c in range(2)]
        rounds = sb("rounds", [1, NI + 1, 4], I32)
        upto = sb("upto", [1, NI + 1])
        fine = sb("fine", [1, 2])
        assert 3 * D <= NT and D <= BE and D <= 6 * NB
        v1 = stats_flat[:, 2 * NB:3 * NB]
        v2 = rstd
        i1 = stats_flat[:, 3 * NB:4 * NB]
        p1 = nmr
        p2 = sb("p2", [P, NB])
        slot_f = stats_flat[:, 0:2 * NB].rearrange("p (k b) -> p k b", k=2)
        slot_i = mv[:, :, :].rearrange("p b s -> p (b s)").bitcast(I32).rearrange("p (k b) -> p k b", k=2)
        part_i = base_i[:, 0:2 * NB].rearrange("p (k b) -> p k b", k=2)
        slot_row = stats_flat[:, 4 * NB:6 * NB]
        slot_tile = in_second[:, 0:2 * NB]
        signed_no = in_second[:, 2 * NB:4 * NB]
        tiles_i = sb("tiles_i", [P, NE], I32)
        tiles_f = sb("tiles_f", [P, NE])
        tiles_c = sb("tiles_c", [P, NE])
        offset = sb("offset", [P, NE])
        expert_f = in_first[0:1, 0:NJ]

        hots = [feat_flat[:, NE * DK * H + s * LM * P:NE * DK * H + (s + 1) * LM * P].rearrange("p (m c) -> p m c", m=LM)
                for s in range(LS)]
        behind_b2 = pool_a[:, NE * D:]
        picks = [t[:, n * LM * NJ:(n + 1) * LM * NJ].rearrange("p (m j) -> p m j", m=LM)
                 for n in range(LS // 2) for t in (behind_b2, onehot_flat)]
        steps_5 = 2 * NB // LM
        assert steps_5 * LM == 2 * NB and NE * DK * H + LS * LM * P <= NB * D and LS // 2 * LM * NJ <= GS * GT * P
        of_slot = target[:, 0:NJ]
        is_empty = target[:, NJ:2 * NJ]
        of_choice = inside[:, 0:2 * NJ].rearrange("p (j k) -> p j k", k=2)
        node_i = base_i[:, 0:NJ]
        b2_sb = pool_a[:, 0:NE * D].rearrange("p (e d) -> p e d", e=NE)
        behind = res[:, :, :].rearrange("p b d -> p (b d)")[:, HK * NE * D:]
        reach = behind[0:1, XS * (R + 2 * D):XS * (R + 2 * D) + NJ * NE].rearrange("p (j e) -> p j e", e=NE)
        row = [behind[:, s * R:(s + 1) * R] for s in range(XS)]
        y_out = [behind[:, XS * R + s * D:XS * R + (s + 1) * D] for s in range(XS)]
        xt = [behind[:, XS * (R + D) + s * D:XS * (R + D) + (s + 1) * D].rearrange("p (k t) -> p k t", k=DK) for s in range(XS)]
        weight = [sb(f"weight{s}", [P, 2]) for s in range(XS)]
        row_id = [sb(f"row_id{s}", [P, 1], I32) for s in range(XS)]
        add_id = [sb(f"add_id{s}", [P, 1], I32) for s in range(XS)]
        hid = [pool_a[:, NE * D + s * H:NE * D + (s + 1) * H].rearrange("p (k t) -> p k t", k=HK) for s in range(XS)]
        assert NE * D + max(XS * H, LS // 2 * LM * NJ) <= GS * GT * R and HK * NE * D + XS * (R + 2 * D) + NJ * NE <= NB * D
        assert 2 * NJ <= NT and NJ <= P

        small_in = sem("small_in")
        dst_in = sem("dst_in")
        src_in = sem("src_in")
        x_in = [sem(f"x_in{c}") for c in range(LC_N)]
        w2_in = sem("w2_in")
        w1_in = sem("w1_in")
        b2_in = sem("b2_in")
        consts = sem("consts")
        zeroed = sem("zeroed")
        agg_zero = sem("agg_zero")
        ring_ones = sem("ring_ones")
        var_ready = sem("var_ready")
        root_ready = sem("root_ready")
        stats_ready = sem("stats_ready")
        feat_ready = sem("feat_ready")
        table_out = sem("table_out")
        base_ready = sem("base_ready")
        base_bc = sem("base_bc")
        miss_sum = sem("miss_sum")
        miss_bc = sem("miss_bc")
        miss_ready = sem("miss_ready")
        rounds_ready = sem("rounds_ready")
        idx_ready = sem("idx_ready")
        gathered = [sem(f"gathered{q}") for q in range(GS)]
        hot_ready = sem("hot_ready")
        summed = [sem(f"summed{q}") for q in range(GS)]
        added = [sem(f"added{q}") for q in range(GS)]
        f_staged = sem("f_staged")
        f_turned = sem("f_turned")
        f_copied = sem("f_copied")
        f_product = sem("f_product")
        res_added = sem("res_added")
        m_idx = sem("m_idx")
        m_gathered = sem("m_gathered")
        m_hot = sem("m_hot")
        m_sum = sem("m_sum")
        m_add = sem("m_add")
        edges_done = sem("edges_done")
        deg_max, deg_inv, mean_set, mean_turned, mean_copied, neigh_done = (sem(n) for n in (
            "deg_max", "deg_inv", "mean_set", "mean_turned", "mean_copied", "neigh_done"))
        x1_done, xn_done, row_done, xn_turned, xn_copied, router_done, logit_done = (sem(n) for n in (
            "x1_done", "xn_done", "row_done", "xn_turned", "xn_copied", "router_done", "logit_done"))
        ln = [{n: sem(f"ln{k}_{n}") for n in ("stats", "mv", "var", "root", "scale", "shift", "out")} for k in range(2)]
        x1_out = sem("x1_out")
        chosen = sem("chosen")
        counted = sem("counted")
        rows_done = sem("rows_done")
        rows_out = sem("rows_out")
        hots_ready = [sem(f"hots_ready{s}") for s in range(LS)]
        picks_ready = [sem(f"picks_ready{s}") for s in range(LS)]
        picked = [sem(f"picked{s}") for s in range(LS)]
        lists_summed = sem("lists_summed")
        lists_ready = sem("lists_ready")
        id_set = sem("id_set")
        weight_set = sem("weight_set")
        row_in = [sem(f"row_in{s}") for s in range(XS)]
        row_free = sem("row_free")
        t_done = sem("t_done")
        xt_ready = sem("xt_ready")
        h_done = sem("h_done")
        w1_set = sem("w1_set")
        h_biased = sem("h_biased")
        gelu_done = sem("gelu_done")
        y_done = sem("y_done")
        y_ready = sem("y_ready")
        y_free = sem("y_free")
        y_biased = sem("y_biased")
        y_added = sem("y_added")
        chain = sem("chain")
        gate = sem("gate")
        gate_pe = sem("gate_pe")
        gate_act = sem("gate_act")
        gate_dve = sem("gate_dve")

        block = ctx.enter_context(nc.Block())

        def rows(t):
            return t.rearrange("(b p) d -> p b d", p=P)

        x_v, table_v, out_v = rows(x), rows(table), rows(out[0:NP, :])
        rows_v = rows(rows_tab[0:NP, :])

        def round_work(engine, i):
            first, count, first_before, count_before = load_values(
                engine, rounds[0:1, bass.ds(i, 1), :].rearrange("p o n -> p (o n)"), NB - 2)
            return (first, count), (first_before, count_before), first + count

        def beside(engine, blocks, *steps):
            first, count = blocks
            with engine.If(count == 1):
                for step in steps:
                    step([(first, 0)])
            with engine.If(count > 1):
                for step in steps:
                    step([(first, 0), (first + 1, 1)])

        def rest(engine, first, *steps):
            with engine.If(first < NB - 2):
                with engine.Fori(0, NB) as b:
                    with engine.If(b >= first):
                        for step in steps:
                            step([(b, 0)])

        def lists_steps(engine, step):
            with engine.Fori(0, steps_5 // LS) as i:
                for s in range(LS):
                    step(i, s)
            for s in range(steps_5 % LS):
                step(steps_5 // LS, s)

        @block.sync
        def _(sp):
            sp.dma_start(dst_i[:, :], dst).then_inc(dst_in, 16)
            for c in range(LC_N):
                s = slice(c * LC, (c + 1) * LC)
                sp.dma_start(res[:, s, :], x_v[:, s, :]).then_inc(x_in[c], 16)
            sp.dma_start(src_sb[:, 0:NT], src).then_inc(src_in, 16)
            for c in range(LC_N):
                s = slice(c * LC, (c + 1) * LC)
                sp.wait_ge(feat_ready, (c + 1) * LC)
                sp.dma_start(table_v[:, s, :], feat[:, s, :]).then_inc(table_out, 16)
            sp.dma_start(ws_sb[:, :, :], w_self.rearrange("(k p) n -> p k n", p=P)).then_inc(small_in, 16)
            sp.dma_start(wn_sb[:, :, :], w_neigh.rearrange("(k p) n -> p k n", p=P)).then_inc(small_in, 16)
            sp.dma_start(bg_sb[:, :], b_gnn).then_inc(small_in, 16)
            sp.dma_start(wr_sb[:, :, :], w_r.rearrange("(k p) n -> p k n", p=P)).then_inc(small_in, 16)
            sp.dma_start(br_sb[:, :], b_r.broadcast_to([P, NE])).then_inc(small_in, 16)
            sp.dma_start(gb_sb[:, 0, :], gamma).then_inc(small_in, 16)
            sp.dma_start(gb_sb[:, 1, :], beta).then_inc(small_in, 16)
            sp.wait_ge(zeroed, 1)
            sp.dma_start(rows_tab[NP:NP + P, :], zrow[:, 0, :]).then_inc(rows_out, 16)
            sp.wait_ge(f_staged, NB)
            sp.wait_ge(gathered[GS - 1], 16 * GT * NI)
            sp.wait_ge(table_out, 16 * LC_N)
            for k in range(DK):
                sp.dma_start(w1_sb[:, k, :, :], w1[:, k * P:(k + 1) * P, :].rearrange("e p h -> p e h")).then_inc(w1_in, 16)
            sp.dma_start(b1_sb[:, :, :], b1).then_inc(w1_in, 16)
            sp.wait_ge(edges_done, 1)
            sp.dma_start(b2_sb, b2.broadcast_to([P, NE * D]).rearrange("p (e d) -> p e d", e=NE)).then_inc(b2_in, 16)
            sp.dma_start(out[NP:NP + P, :], zrow[:, 0, 0:D]).then_inc(x1_out, 16)
            sp.wait_ge(x1_done, NB)
            for c in range(LC_N):
                s = slice(c * LC, (c + 1) * LC)
                sp.dma_start(out_v[:, s, :], res[:, s, :]).then_inc(x1_out, 16)
            sp.wait_ge(ln[0]["out"], NB)
            sp.wait_ge(x1_out, 16 * (LC_N + 1))
            for k in range(HK):
                sp.dma_start(w2_sb[:, k, :, :], w2[:, k * P:(k + 1) * P, :].rearrange("e p d -> p e d")).then_inc(w2_in, 16)
            sp.wait_ge(rows_done, 1)
            for c in range(LC_N):
                s = slice(c * LC, (c + 1) * LC)
                sp.dma_start(rows_v[:, s, :], agg[:, s, :]).then_inc(rows_out, 16)
            sp.wait_ge(rows_out, 16 * (LC_N + 1))

        @block.gpsimd
        def _(pool):
            pool.memset(ones[:, :], 1.0).then_inc(consts, 1)
            pool.iota(iota[:, :], [[1, P]], base=0, channel_multiplier=0, allow_small_or_imprecise_dtypes=True).then_inc(consts, 1)
            pool.iota(iota_p[:, :], [[0, 1]], base=0, channel_multiplier=1, allow_small_or_imprecise_dtypes=True).then_inc(consts, 1)
            pool.iota(node_no[:, :], [[P, NB]], base=1, channel_multiplier=1, allow_small_or_imprecise_dtypes=True).then_inc(consts, 1)
            pool.iota(empty_no[:, :], [[0, 1]], base=NP + 1, channel_multiplier=1, allow_small_or_imprecise_dtypes=True).then_inc(consts, 1)
            pool.wait_ge(consts, 1)
            pool.affine_select(out=ident[:, :], in_=ones[:, :], compare_op=ALU.is_equal, fill=0.0,
                               base=0, pattern=[[-1, P]], channel_multiplier=1).then_inc(consts, 1)
            pool.affine_select(out=upper[:, :], in_=ones[:, :], compare_op=ALU.is_gt, fill=0.0,
                               base=0, pattern=[[1, P]], channel_multiplier=-1).then_inc(consts, 1)
            pool.memset(src_sb[:, NT:], 0).then_inc(consts, 1)
            pool.memset(zrow[:, :, :], 0.0).then_inc(zeroed, 1)
            pool.memset(ring[:, :, D:D + 1], 1.0).then_inc(ring_ones, 1)
            pool.memset(agg[:, :, :], 0.0).then_inc(agg_zero, 1)
            pool.wait_ge(table_out, 16 * LC_N)
            with pool.Fori(0, NI) as i:
                for q in range(GS):
                    pool.wait_ge(idx_ready, GS * i + q + 1)
                    pool.wait_ge(summed[q], i + 1)
                    pool.sem_inc(gate, 1)
                    for t in range(GT):
                        pool.indirect_dma_start(ring[:, q * GT + t, 0:D], None, table,
                                                bass.IndirectOffsetOnAxis(idx[:, q, t:t + 1], 0)).then_inc(gathered[q], 16)
            pool.wait_ge(miss_ready, 1)
            pool.wait_ge(idx_ready, NG + GS - 1)
            n_miss = pool.value_load(missed_i[0:1, 0:1], min_val=0, max_val=NT * P)
            for q in range(GS):
                pool.wait_ge(summed[q], NI + 1)
            with pool.If(n_miss > 0):
                with pool.Fori(0, NT) as t:
                    pool.wait_ge(m_sum, NB * t + 1)
                    pool.tensor_copy(idx[:, 0, 0:1], src_sb[:, bass.ds(t, 1)]).then_inc(m_idx, 1)
                    pool.wait_ge(m_idx, t + 1)
                    pool.sem_inc(gate, 1)
                    pool.indirect_dma_start(ring[:, 0, 0:D], None, table,
                                            bass.IndirectOffsetOnAxis(idx[:, 0, 0:1], 0)).then_inc(m_gathered, 16)

            def copy_id(to, j, n):
                pool.tensor_copy(to[:, :], node_i[:, bass.ds(j, 1)]).then_inc(id_set, 1)
                pool.wait_ge(id_set, n)
                pool.sem_inc(gate, 1)

            def gather_rows(j, s, n):
                copy_id(row_id[s], j, n)
                pool.indirect_dma_start(row[s], None, rows_tab, bass.IndirectOffsetOnAxis(row_id[s][:, :], 0)).then_inc(row_in[s], 16)

            def add_rows(j, s, n):
                copy_id(add_id[s], j, n)
                pool.wait_ge(y_ready, j + 1)
                pool.sem_inc(gate, 1)
                pool.indirect_dma_start(out, bass.IndirectOffsetOnAxis(add_id[s][:, :], 0),
                                        y_out[s], None, compute_op=ALU.add).then_inc(y_added, 16)

            def added_before(j):
                pool.wait_ge(y_added, 16 * j)
                pool.sem_inc(y_free, 1)

            def pool_step(j, s, first=False):
                pool.wait_ge(row_free, j + 2)
                gather_rows(j + XS + 1, (s + 1) % XS, 2 * j + XS + 2)
                if not first:
                    added_before(j)
                add_rows(j, s, 2 * j + XS + 3)

            pool.wait_ge(lists_ready, 1)
            pool.wait_ge(rows_out, 16 * (LC_N + 1))
            pool.wait_ge(x1_out, 16 * (LC_N + 1))
            for j in range(XS):
                gather_rows(j, j, j + 1)
            pool.wait_ge(row_free, 1)
            gather_rows(XS, 0, XS + 1)
            for j in range(XS):
                pool_step(j, j, first=(j == 0))
            with pool.Fori(1, NJ // XS - 2) as i:
                for s in range(XS):
                    pool_step(XS * i + s, s)
            for j in range(NJ - 2 * XS, NJ - XS - 1):
                pool_step(j, j % XS)
            for j in range(NJ - XS - 1, NJ):
                added_before(j)
                add_rows(j, j % XS, NJ + 1 + j)
            pool.wait_ge(y_added, 16 * NJ)

        @block.scalar
        def _(act):
            def root(lo, hi, n):
                act.wait_ge(var_ready, n)
                act.activation(rstd[:, lo:hi], rstd[:, lo:hi], ACT.Sqrt).then_inc(root_ready, 1)

            act.sem_inc(f_copied, 1)
            act.sem_inc(row_done, 1)
            act.sem_inc(mean_copied, 1)
            for c in range(LC_N):
                root(c * LC, (c + 1) * LC, c + 1)
                act.wait_ge(stats_ready, c + 1)
                for b in range(c * LC, (c + 1) * LC):
                    act.activation(feat[:, b, :], res[:, b, :], ACT.Identity, bias=nmr[:, b:b + 1],
                                   scale=rstd[:, b:b + 1]).then_inc(feat_ready, 1)
            act.wait_ge(feat_ready, NB)
            act.wait_ge(src_in, 16)

            def mean(blocks):
                for b, c in blocks:
                    act.wait_ge(deg_inv, b + 1)
                    act.sem_inc(gate_act, 1)
                    act.activation(mean_rows[c], agg[:, bass.ds(b, 1), 0:D], ACT.Copy, scale=ninv[c][:, 0:1]).then_inc(mean_set, 1)

            def mean_transposed(blocks):
                act.wait_ge(mean_turned, blocks[-1][0] + 1)
                for b, c in blocks:
                    act.copy(mean_t[c], bank[5][:, c * D:(c + 1) * D].rearrange("p (k t) -> p k t", k=DK)).then_inc(mean_copied, 1)

            def normal(k, blocks):
                if k == 1:
                    act.wait_ge(row_done, blocks[0][0] + 1)
                for b, c in blocks:
                    act.wait_ge(ln[k]["var"], b + 1)
                    act.activation(nscale[c][:, :], nscale[c][:, :], ACT.Sqrt).then_inc(ln[k]["root"], 1)
                for b, c in blocks:
                    act.wait_ge(ln[k]["shift"], b + 1)
                    act.sem_inc(gate_act, 1)
                    if k == 0:
                        act.activation(agg[:, bass.ds(b, 1), 0:D], res[:, bass.ds(b, 1), :], ACT.Identity,
                                       bias=nshift[c][:, 0:1], scale=nscale[c][:, 0:1]).then_inc(ln[0]["out"], 1)
                    else:
                        act.activation(normal_rows[c], agg[:, bass.ds(b, 1), 0:D], ACT.Identity, bias=nshift[c][:, 0:1],
                                       scale=nscale[c][:, 0:1]).then_inc(xn_done, 1)

            def normal_transposed(blocks):
                act.wait_ge(xn_turned, blocks[-1][0] + 1)
                for b, c in blocks:
                    for k in range(DK):
                        last = act.activation(normal_t[c][:, k, :], bank[7][:, c * D + k * P:c * D + (k + 1) * P], ACT.Identity,
                                              bias=gb_sb[:, 1, k:k + 1], scale=gb_sb[:, 0, k:k + 1])
                    last.then_inc(xn_copied, 1)
                for b, c in blocks:
                    act.activation(agg[:, bass.ds(b, 1), 0:D], normal_rows[c], ACT.Copy).then_inc(row_done, 1)

            def normal_0(blocks):
                normal(0, blocks)

            def normal_1(blocks):
                normal(1, blocks)

            def stage_idx(i, q):
                act.wait_ge(summed[q], i + 1)
                act.copy(idx[:, q, :], src_sb[:, bass.ds(i * GS * GT + q * GT, GT)]).then_inc(idx_ready, 1)

            act.wait_ge(consts, 8)
            stage_idx(0, 0)
            stage_idx(0, 1)
            stage_idx(0, 2)
            act.wait_ge(rounds_ready, 1)
            last_work = round_work(mybir.EngineType.Activation, NI)
            with act.Fori(0, NI) as i:
                now, before, begun = round_work(mybir.EngineType.Activation, i)
                for q in range(GS):
                    stage_idx(i + (q + 3) // GS, (q + 3) % GS)
                    if q == 0:
                        act.wait_ge(f_turned, i + 1)
                        act.copy(stage[:, :], feat[:, bass.ds(i, 1), :]).then_inc(f_staged, 1)
                        beside(act, now, mean)
                        beside(act, before, normal_1)
                    if q == 1:
                        beside(act, now, mean_transposed)
                    if q == 2:
                        act.wait_ge(f_turned, i + 2)
                        act.wait_ge(f_product, i + 1)
                        act.copy(stage_f[:, :, :], bank[4][:, 0:D].rearrange("p (k t) -> p k t", k=DK)).then_inc(f_copied, 1)
                        beside(act, before, normal_transposed)
                        beside(act, now, normal_0)
            now, before, begun = last_work
            beside(act, now, mean)
            beside(act, before, normal_1)
            beside(act, now, mean_transposed)
            beside(act, before, normal_transposed)
            beside(act, now, normal_0, normal_1, normal_transposed)
            rest(act, now[0], mean, mean_transposed, normal_0, normal_1, normal_transposed)
            act.wait_ge(chosen, 1)
            act.activation(p2[:, :], v2[:, :], ACT.Exp).then_inc(chosen, 1)
            def sign_picks(i, s):
                act.wait_ge(hots_ready[s], i + 1)
                act.sem_inc(gate_act, 1)
                for m in range(LM):
                    last = act.activation(picks[s][:, m, :], picks[s][:, m, :], ACT.Copy,
                                          scale=signed_no[:, bass.ds(LM * LS * i + LM * s + m, 1)])
                last.then_inc(picks_ready[s], 1)

            lists_steps(act, sign_picks)
            act.wait_ge(w1_in, 16 * (DK + 1))
            act.wait_ge(lists_ready, 1)

            def set_w1(j, s, e):
                if not isinstance(j, int) or j >= XS:
                    act.wait_ge(h_done, j - XS + 1)
                act.sem_inc(gate_act, 1)
                act.copy(w1_of[s], w1_sb[:, :, bass.ds(e, 1), :].rearrange("p k o h -> p k (o h)")).then_inc(w1_set, 1)

            def gelu(j, s):
                act.wait_ge(h_biased, j + 1)
                act.activation(hid[s], hid[s], ACT.Gelu).then_inc(gelu_done, 1)

            def act_experts(i):
                return load_values(mybir.EngineType.Activation, experts[0:1, bass.ds(i, 1), :].rearrange("p o s -> p (o s)"),
                                   NE - 1, **unchecked)

            e = act_experts(0)
            for j in range(XS):
                set_w1(j, j, e[j + 1])
            with act.Fori(1, NJ // XS) as i:
                e = act_experts(i)
                for s in range(XS):
                    gelu(XS * (i - 1) + s, s)
                    set_w1(XS * i + s, s, e[s + 1])
            for j in range(NJ - XS, NJ):
                gelu(j, j % XS)

        @block.tensor
        def _(pe):
            for s in (*picked, *summed, f_turned, f_product, m_sum, neigh_done):
                pe.sem_inc(s, 1)
            pe.wait_ge(consts, 7)
            pe.wait_ge(base_ready, 1)
            pe.matmul(bank[6][:, 0:NG], ones[0:1, :], base_f, start=True, stop=True).then_inc(base_bc, 1)
            pe.wait_ge(miss_sum, 1)
            pe.matmul(bank[7][0:1, 0:1], n_missed[:, 0:1], ones[:, 0:1], start=True, stop=True).then_inc(miss_bc, 1)
            pe.wait_ge(small_in, 16 * 7)
            pe.wait_ge(ring_ones, 1)

            def turn(to, block):
                for k in range(DK):
                    last = pe.transpose(to[:, k * P:(k + 1) * P], block[:, k * P:(k + 1) * P], ident[:, :])
                return last

            def product(to, turned, weights):
                for k in range(DK):
                    last = pe.matmul(to, turned[:, k, :], weights[:, k, :], start=(k == 0), stop=(k == DK - 1))
                return last

            def turn_mean(read, blocks):
                pe.wait_ge(logit_done, read + 1)
                for b, c in blocks:
                    pe.wait_ge(mean_set, b + 1)
                    turn(bank[5][:, c * D:(c + 1) * D], mean_rows[c]).then_inc(mean_turned, 1)

            def neighbours(blocks):
                for b, c in blocks:
                    pe.wait_ge(mean_copied, b + 2)
                    product(bank[6][:, c * D:(c + 1) * D], mean_t[c], wn_sb).then_inc(neigh_done, 1)

            def turn_normal(blocks):
                for b, c in blocks:
                    pe.wait_ge(xn_done, b + 1)
                    turn(bank[7][:, c * D:(c + 1) * D], normal_rows[c]).then_inc(xn_turned, 1)

            def router(begun, blocks):
                pe.wait_ge(mean_copied, begun + 1)
                for b, c in blocks:
                    pe.wait_ge(xn_copied, b + 1)
                    product(bank[5][:, c * NE:(c + 1) * NE], normal_t[c], wr_sb).then_inc(router_done, 1)

            pe.wait_ge(rounds_ready, 1)
            last_work = round_work(mybir.EngineType.PE, NI)
            with pe.Fori(0, NI) as i:
                now, before, begun = round_work(mybir.EngineType.PE, i)
                for q in range(GS):
                    pe.wait_ge(hot_ready, GS * i + q + 1)
                    pe.wait_ge(gathered[q], 16 * GT * (i + 1))
                    pe.wait_ge(added[q], i + 1)
                    for t in range(GT):
                        last = pe.matmul(bank[q][:, 0:D + 1], onehot[:, q, t, :], ring[:, q * GT + t, 0:D + 1],
                                         start=(t == 0), stop=(t == GT - 1))
                    last.then_inc(summed[q], 1)
                    if q == 1:
                        pe.wait_ge(f_staged, i + 1)
                        pe.wait_ge(f_copied, i + 1)
                        pe.wait_ge(res_added, i + 1)
                        turn(bank[4], stage).then_inc(f_turned, 1)
                        beside(pe, now, lambda blocks: turn_mean(before[0], blocks))
                    if q == 2:
                        beside(pe, now, neighbours)
                        beside(pe, before, turn_normal)
                    if q == 3:
                        pe.wait_ge(f_copied, i + 2)
                        for k in range(DK):
                            pe.matmul(bank[4][:, D:2 * D], stage_f[:, k, :], ws_sb[:, k, :], start=(k == 0), stop=False)
                        pe.matmul(bank[4][:, D:2 * D], ones[0:1, :], bg_sb[:, :], start=False, stop=True).then_inc(f_product, 1)
                        beside(pe, before, lambda blocks: router(begun, blocks))
            pe.wait_ge(miss_ready, 1)
            n_miss = pe.value_load(missed_i[0:1, 0:1], min_val=0, max_val=NT * P)
            with pe.If(n_miss > 0):
                with pe.Fori(0, NT) as t:
                    pe.wait_ge(m_gathered, 16 * (t + 1))
                    pe.sem_inc(gate_pe, 1)
                    with pe.Fori(0, NB) as w:
                        pe.wait_ge(m_hot, NB * t + w + 1)
                        pe.wait_ge(m_add, NB * t + w + 1)
                        pe.matmul(bank[0][:, 0:D + 1], onehot[:, 0, 0, :], ring[:, 0, 0:D + 1],
                                  start=True, stop=True).then_inc(m_sum, 1)
            now, before, begun = last_work
            beside(pe, now, lambda blocks: turn_mean(before[0], blocks), neighbours)
            beside(pe, before, turn_normal, lambda blocks: router(begun, blocks))
            beside(pe, now, turn_normal, lambda blocks: router(begun, blocks))
            rest(pe, now[0], lambda blocks: turn_mean(blocks[0][0], blocks), neighbours, turn_normal, lambda blocks: router(blocks[-1][0] + 1, blocks))
            pe.wait_ge(chosen, 3)
            pe.matmul(bank[6][:, 0:BE], upper[:, :], missed[:, 0:BE], start=True, stop=True).then_inc(counted, 1)
            pe.matmul(bank[7][:, 0:BE], ones[:, :], missed[:, 0:BE], start=True, stop=True).then_inc(counted, 1)
            def zeros_product(**flags):
                return pe.matmul(bank[4][:, 0:NJ], zrow[:, 0, 0:P], iota[:, 0:NJ], **flags)

            pe.wait_ge(zeroed, 1)
            zeros_product(start=True, stop=False)

            def place(i, s):
                pe.wait_ge(picks_ready[s], i + 1)
                for m in range(LM):
                    last = pe.matmul(bank[4][:, 0:NJ], hots[s][:, m, :], picks[s][:, m, :], start=False, stop=False)
                last.then_inc(picked[s], 1)

            lists_steps(pe, place)
            zeros_product(start=False, stop=True).then_inc(lists_summed, 1)
            pe.wait_ge(lists_ready, 1)
            pe.wait_ge(w1_in, 16 * (DK + 1))
            pe.wait_ge(w2_in, 16 * HK)
            pe.wait_ge(b2_in, 16)

            def turn_rows(j, n, s):
                pe.wait_ge(row_in[s], 16 * (n + 1))
                if not isinstance(j, int) or j > 0:
                    pe.wait_ge(xt_ready, j)
                turn(bank[0], row[s]).then_inc(t_done, 1)

            def hidden(j, s):
                pe.wait_ge(xt_ready, j + 1)
                pe.wait_ge(w1_set, j + 1)
                if not isinstance(j, int) or j > 0:
                    pe.wait_ge(h_biased, j)
                for c in range(HK):
                    for k in range(DK):
                        last = pe.matmul(bank[1][:, c * P:(c + 1) * P], w1_of[s][:, k, c * P:(c + 1) * P], xt[s][:, k, :],
                                         start=(k == 0), stop=(k == DK - 1))
                last.then_inc(h_done, 1)

            def results(j, s, e):
                pe.wait_ge(gelu_done, j + 1)
                if not isinstance(j, int) or j > 0:
                    pe.wait_ge(y_biased, j)
                for k in range(HK):
                    last = pe.matmul(bank[3][:, 0:D], hid[s][:, k, :], w2_sb[:, k, bass.ds(e, 1), :], start=(k == 0), stop=(k == HK - 1))
                last.then_inc(y_done, 1)

            def pe_step(j, n, s, e):
                turn_rows(j + 1, n + (s + 1) // XS, (s + 1) % XS)
                hidden(j, s)
                results(j - 1, (s - 1) % XS, e[s])

            def pe_experts(i):
                return load_values(mybir.EngineType.PE, experts[0:1, bass.ds(i, 1), :].rearrange("p o s -> p (o s)"), NE - 1, **unchecked)

            e = pe_experts(0)
            turn_rows(0, 0, 0)
            turn_rows(1, 0, 1)
            hidden(0, 0)
            for j in range(1, XS):
                pe_step(j, 0, j, e)
            with pe.Fori(1, NJ // XS - 1) as i:
                e = pe_experts(i)
                for s in range(XS):
                    pe_step(XS * i + s, i, s, e)
            e = pe_experts(NJ // XS - 1)
            for j in range(NJ - XS, NJ - 1):
                pe_step(j, j // XS, j % XS, e)
            hidden(NJ - 1, XS - 1)
            results(NJ - 2, (NJ - 2) % XS, e[XS - 1])
            results(NJ - 1, (NJ - 1) % XS, e[XS])

        @block.vector
        def _(dve):
            for s in (*added, res_added, m_add, logit_done):
                dve.sem_inc(s, 1)
            links = [0]

            def link(ins):
                links[0] += 1
                ins.then_inc(chain, 1)
                dve.wait_ge(chain, links[0])

            def scale_and_shift(lo, hi, n):
                dve.tensor_scalar(rstd[:, lo:hi], mv[:, lo:hi, 1], EPS, None, ALU.add).then_inc(var_ready, 1)
                dve.wait_ge(root_ready, n)
                link(dve.reciprocal(rstd[:, lo:hi], rstd[:, lo:hi]))
                return dve.scalar_tensor_tensor(out=nmr[:, lo:hi], in0=mv[:, lo:hi, 0], scalar=-1.0,
                                                in1=rstd[:, lo:hi], op0=ALU.mult, op1=ALU.mult)

            dve.wait_ge(dst_in, 16)
            dve.tensor_copy(base_f, dst_i[0:1, :].rearrange("p (g t) -> p g t", t=GT)[:, :, 0]).then_inc(base_ready, 1)
            for c in range(LC_N):
                dve.wait_ge(x_in[c], 16)
                for b in range(c * LC, (c + 1) * LC):
                    last = dve.bn_stats(stats[:, b, :], res[:, b, :])
                link(last)
                for b in range(c * LC, (c + 1) * LC):
                    last = dve.bn_aggr(mv[:, b, :], stats[:, b, :])
                link(last)
                scale_and_shift(c * LC, (c + 1) * LC, c + 1).then_inc(stats_ready, 1)
            dve.wait_ge(base_bc, 1)
            dve.wait_ge(consts, 7)
            link(dve.tensor_copy(base_i[:, :], bank[6][:, 0:NG]))
            by_group = inside[:, :].rearrange("p (g t) -> p g t", t=GT)
            link(dve.tensor_tensor(by_group, dst_i[:, :].rearrange("p (g t) -> p g t", t=GT),
                                   base_i[:, :].unsqueeze(2).broadcast_to([P, NG, GT]), ALU.subtract))
            link(dve.tensor_scalar(missed[:, :], inside[:, :], 0.0, None, ALU.is_ge))
            link(dve.tensor_scalar(target, inside[:, :], float(P), None, ALU.is_lt))
            link(dve.tensor_tensor(inside[:, :], missed[:, :], target, ALU.mult))
            link(dve.tensor_scalar(target, inside[:, :], -1.0, 1.0, ALU.mult, ALU.add))
            link(dve.tensor_reduce(n_missed[:, 0:1], target, AX.X, ALU.add))
            down = onehot_flat[0:1, 0:NG]
            link(dve.memset(down, 0.0))
            link(dve.tensor_tensor(down[:, 1:NG], base_i[0:1, 1:NG], base_i[0:1, 0:NG - 1], ALU.is_lt))
            link(dve.tensor_reduce(fine[:, 0:1], down, AX.X, ALU.add))
            dve.tensor_tensor(n_missed[0:1, 0:1], n_missed[0:1, 0:1], fine[:, 0:1], ALU.add).then_inc(miss_sum, 1)
            link(dve.scalar_tensor_tensor(out=missed[:, :], in0=dst_i[:, :], scalar=1.0, in1=target,
                                          op0=ALU.add, op1=ALU.mult))
            link(dve.tensor_scalar(missed[:, :], missed[:, :], -1.0, None, ALU.add))
            link(dve.tensor_scalar(dst_i[:, :], dst_i[:, :], P - 1, None, ALU.bitwise_and))
            link(dve.scalar_tensor_tensor(out=target, in0=dst_i[:, :], scalar=1.0, in1=inside[:, :],
                                          op0=ALU.add, op1=ALU.mult))
            link(dve.tensor_scalar(target, target, -1.0, None, ALU.add))
            link(dve.tensor_scalar(block_i[:, :], base_i[0:1, :], 7, None, ALU.arith_shift_right))
            link(dve.tensor_scalar(base_i[:, :], base_i[:, :], P - 1, None, ALU.bitwise_and))
            link(dve.tensor_scalar(in_second[:, :], base_i[:, :], iota_p[:, 0:1], None, ALU.is_gt))
            link(dve.tensor_scalar(in_first[:, :], in_second[:, :], -1.0, 1.0, ALU.mult, ALU.add))
            dve.wait_ge(miss_bc, 1)
            dve.tensor_copy(missed_i[:, :], bank[7][0:1, 0:1]).then_inc(miss_ready, 1)
            link(dve.tensor_scalar(fine[:, 1:2], bank[7][0:1, 0:1], 0.0, None, ALU.is_equal))
            link(dve.tensor_scalar(upto[:, 1:NI + 1], block_i[:, :].rearrange("p (i q) -> p i q", q=GS)[:, :, 0],
                                   fine[:, 1:2], None, ALU.mult))
            link(dve.scalar_tensor_tensor(out=upto[:, 1:NI + 1], in0=upto[:, 1:NI + 1], scalar=float(NB - 2),
                                          in1=iota[0:1, 0:NI], op0=ALU.min, op1=ALU.min))
            two = onehot_flat[0:1, 0:NI]
            link(dve.memset(two, 2.0))
            link(dve.memset(upto[:, 0:1], 0.0))
            link(dve.tensor_tensor_scan(upto[:, 1:NI + 1], two, upto[:, 1:NI + 1], 0.0, ALU.add, ALU.min))
            link(dve.memset(rounds[:, :, :], 0))
            dve.tensor_copy(rounds[:, :, 0], upto[:, :])
            dve.tensor_copy(rounds[:, 1:, 2], upto[:, 0:NI])
            dve.tensor_tensor(rounds[:, 0:NI, 1], upto[:, 1:NI + 1], upto[:, 0:NI], ALU.subtract)
            dve.tensor_tensor(rounds[:, 1:, 3], upto[:, 1:NI + 1], upto[:, 0:NI], ALU.subtract)
            dve.tensor_scalar(rounds[:, NI, 1:2], upto[:, NI:NI + 1], float(NB - 2), 2.0, ALU.is_equal,
                              ALU.mult).then_inc(rounds_ready, 1)
            dve.wait_ge(agg_zero, 1)

            def one_hots(i, q):
                dve.wait_ge(summed[q], i + 1)
                dve.tensor_tensor(onehot[:, q, :, :], iota[:, :].unsqueeze(1).broadcast_to([P, GT, P]),
                                  target_all[:, bass.ds(i * GS * GT + q * GT, GT)].unsqueeze(2).broadcast_to([P, GT, P]),
                                  ALU.is_equal).then_inc(hot_ready, 1)

            def add_sums(i, q, blk):
                g = i * GS + q
                dve.wait_ge(summed[q], i + 2)
                if q:
                    dve.wait_ge(added[q - 1], i + 2)
                else:
                    dve.wait_ge(added[GS - 1], i + 1)
                for n, mask in ((0, in_first), (1, in_second)):
                    a = agg[:, bass.ds(blk + n, 1), 0:D + 1].rearrange("p o d -> p (o d)")
                    last = dve.scalar_tensor_tensor(out=a, in0=bank[q][:, 0:D + 1], scalar=mask[:, bass.ds(g, 1)],
                                                    in1=a, op0=ALU.mult, op1=ALU.add)
                last.then_inc(added[q], 1)

            dve.memset(target_all[:, NT:], -1.0).then_inc(chain, 1)
            links[0] += 1
            dve.wait_ge(chain, links[0])
            one_hots(0, 0)
            one_hots(0, 1)
            dve.wait_ge(rounds_ready, 1)
            last_work = round_work(mybir.EngineType.DVE, NI)

            def degrees(blocks):
                for b, c in blocks:
                    dve.tensor_scalar(ninv[c][:, :], agg[:, bass.ds(b, 1), D], 1.0, None, ALU.max).then_inc(deg_max, 1)
                for b, c in blocks:
                    dve.wait_ge(deg_max, b + 1)
                    dve.reciprocal(ninv[c][:, :], ninv[c][:, :]).then_inc(deg_inv, 1)

            def moments(k, b, c, source):
                dve.bn_stats(nstats[c][:, :], source).then_inc(ln[k]["stats"], 1)
                dve.wait_ge(ln[k]["stats"], b + 1)
                dve.sem_inc(gate_dve, 1)
                dve.bn_aggr(nmv[c][:, :], nstats[c][:, :]).then_inc(ln[k]["mv"], 1)
                dve.wait_ge(ln[k]["mv"], b + 1)
                dve.tensor_scalar(nscale[c][:, :], nmv[c][:, 1:2], EPS, None, ALU.add).then_inc(ln[k]["var"], 1)

            def scales(k, blocks):
                for b, c in blocks:
                    dve.wait_ge(ln[k]["root"], b + 1)
                    dve.reciprocal(nscale[c][:, :], nscale[c][:, :]).then_inc(ln[k]["scale"], 1)
                for b, c in blocks:
                    dve.wait_ge(ln[k]["scale"], b + 1)
                    dve.scalar_tensor_tensor(out=nshift[c][:, :], in0=nmv[c][:, 0:1], scalar=-1.0, in1=nscale[c][:, :],
                                             op0=ALU.mult, op1=ALU.mult).then_inc(ln[k]["shift"], 1)

            def x1_sums(blocks):
                dve.wait_ge(neigh_done, blocks[-1][0] + 2)
                for b, c in blocks:
                    r = res[:, bass.ds(b, 1), :].rearrange("p o d -> p (o d)")
                    dve.tensor_tensor(r, r, bank[6][:, c * D:(c + 1) * D], ALU.add).then_inc(x1_done, 1)
                for b, c in blocks:
                    dve.wait_ge(x1_done, b + 1)
                    dve.sem_inc(gate_dve, 1)
                    moments(0, b, c, res[:, bass.ds(b, 1), :].rearrange("p o d -> p (o d)"))
                scales(0, blocks)

            def second_moments(blocks):
                for b, c in blocks:
                    dve.wait_ge(ln[0]["out"], b + 1)
                    dve.sem_inc(gate_dve, 1)
                    moments(1, b, c, agg[:, bass.ds(b, 1), 0:D].rearrange("p o d -> p (o d)"))
                scales(1, blocks)

            def add_router_bias(blocks):
                dve.wait_ge(router_done, blocks[-1][0] + 1)
                for b, c in blocks:
                    dve.tensor_tensor(inside[:, bass.ds(b * NE, NE)], bank[5][:, c * NE:(c + 1) * NE], br_sb[:, :],
                                      ALU.add).then_inc(logit_done, 1)

            with dve.Fori(0, NI) as i:
                blocks = load_values(mybir.EngineType.DVE, block_i[0:1, bass.ds(i * GS, GS)], NB - 1, **unchecked)
                now, before, begun = round_work(mybir.EngineType.DVE, i)
                for q in range(GS):
                    one_hots(i + (q + 2) // GS, (q + 2) % GS)
                    add_sums(i, q, blocks[q])
                    if q == 0:
                        beside(dve, now, degrees)
                        beside(dve, before, second_moments)
                    if q == 2:
                        beside(dve, now, x1_sums)
                    if q == 3:
                        beside(dve, before, add_router_bias)
                dve.wait_ge(f_product, i + 2)
                r = res[:, bass.ds(i, 1), :].rearrange("p o d -> p (o d)")
                dve.tensor_tensor(r, r, bank[4][:, D:2 * D], ALU.add).then_inc(res_added, 1)
            n_miss = dve.value_load(missed_i[0:1, 0:1], min_val=0, max_val=NT * P)
            dve.wait_ge(added[GS - 1], NI + 1)
            with dve.If(n_miss > 0):
                with dve.Fori(0, NT) as t:
                    with dve.Fori(0, NB) as w:
                        dve.wait_ge(m_sum, NB * t + w + 1)
                        dve.tensor_scalar(onehot[:, 0, 0, :], iota[:, :], missed[:, bass.ds(t, 1)], None,
                                          ALU.is_equal).then_inc(m_hot, 1)
                        dve.wait_ge(m_hot, NB * t + w + 1)
                        m = missed[:, bass.ds(t, 1)]
                        dve.tensor_scalar(m, m, float(-P), None, ALU.add)
                        dve.wait_ge(m_sum, NB * t + w + 2)
                        a = agg[:, bass.ds(w, 1), 0:D + 1].rearrange("p o d -> p (o d)")
                        dve.tensor_tensor(a, a, bank[0][:, 0:D + 1], ALU.add).then_inc(m_add, 1)
                        dve.wait_ge(m_add, NB * t + w + 2)
            dve.sem_inc(edges_done, 1)
            dve.wait_ge(res_added, NB + 1)
            now, before, begun = last_work
            beside(dve, now, degrees)
            beside(dve, before, second_moments)
            beside(dve, now, x1_sums)
            beside(dve, before, add_router_bias)
            beside(dve, now, second_moments, add_router_bias)
            rest(dve, now[0], degrees, x1_sums, second_moments, add_router_bias)
            dve.wait_ge(logit_done, NB + 1)

            def over_e(t):
                return t.unsqueeze(2).broadcast_to([P, NB, NE])

            iota_e = iota[:, 0:NE].unsqueeze(1).broadcast_to([P, NB, NE])

            def choose(values, top, choice):
                link(dve.tensor_reduce(top, values, AX.X, ALU.max))
                link(dve.tensor_tensor(choice, values, over_e(top), ALU.is_lt))
                link(dve.scalar_tensor_tensor(out=choice, in0=choice, scalar=float(NE), in1=iota_e, op0=ALU.mult, op1=ALU.add))
                link(dve.tensor_reduce(i1, choice, AX.X, ALU.min))
                link(dve.tensor_tensor(choice, iota_e, over_e(i1), ALU.is_equal))

            choose(logits, v1, choice1)
            link(dve.tensor_scalar(work, choice1, -1.0, 1.0, ALU.mult, ALU.add))
            link(dve.tensor_tensor(work, work, logits, ALU.mult))
            link(dve.scalar_tensor_tensor(out=work, in0=choice1, scalar=LOWEST, in1=work, op0=ALU.mult, op1=ALU.add))
            choose(work, v2[:, :], choice2)
            dve.wait_ge(row_done, NB + 1)
            link(dve.tensor_tensor(both, choice1, choice2, ALU.add))
            dve.tensor_tensor(v2[:, :], v2[:, :], v1, ALU.subtract).then_inc(chosen, 1)
            dve.wait_ge(chosen, 2)
            dve.tensor_scalar(v1, p2[:, :], 1.0, None, ALU.add).then_inc(chosen, 1)
            dve.wait_ge(chosen, 3)
            link(dve.reciprocal(p1[:, :], v1))
            link(dve.tensor_tensor(p2[:, :], p2[:, :], p1[:, :], ALU.mult))
            dve.tensor_copy(agg[:, 0:NB, D], p1[:, :])
            dve.tensor_copy(agg[:, 0:NB, D + 1], p2[:, :]).then_inc(rows_done, 1)
            dve.wait_ge(counted, 2)
            link(dve.tensor_copy(total, bank[7][:, 0:BE].rearrange("p (b e) -> p b e", e=NE)))
            ones_b = ones[:, 0:NB]
            for e in range(NE):
                last = dve.tensor_tensor_scan(incl[:, :, e], ones_b, total[:, :, e], 0.0, ALU.mult, ALU.add)
            link(last)
            link(dve.tensor_scalar(tiles_i[:, :], incl[:, NB - 1, :], float(P - 1), None, ALU.add))
            link(dve.tensor_scalar(tiles_i[:, :], tiles_i[:, :], 7, None, ALU.arith_shift_right))
            link(dve.tensor_copy(tiles_f[:, :], tiles_i[:, :]))
            link(dve.tensor_tensor_scan(tiles_c[:, :], ones[:, 0:NE], tiles_f[:, :], 0.0, ALU.mult, ALU.add))
            link(dve.tensor_tensor(offset[:, :], tiles_c[:, :], tiles_f[:, :], ALU.subtract))
            link(dve.tensor_tensor(work, incl[:, :, :], total, ALU.subtract))
            link(dve.tensor_tensor(work, work, bank[6][:, 0:BE].rearrange("p (b e) -> p b e", e=NE), ALU.add))
            link(dve.scalar_tensor_tensor(out=work, in0=offset[:, :].unsqueeze(1).broadcast_to([P, NB, NE]), scalar=float(P),
                                          in1=work, op0=ALU.mult, op1=ALU.add))
            for k, choice in ((0, choice1), (1, choice2)):
                link(dve.tensor_tensor(total, choice, work, ALU.mult))
                link(dve.tensor_reduce(slot_f[:, k, :], total, AX.X, ALU.add))
            link(dve.tensor_copy(slot_i[:, :, :], slot_f))
            link(dve.tensor_scalar(part_i[:, :, :], slot_i[:, :, :], P - 1, None, ALU.bitwise_and))
            link(dve.tensor_copy(slot_row, part_i[:, :, :].rearrange("p k b -> p (k b)")))
            link(dve.tensor_scalar(slot_i[:, :, :], slot_i[:, :, :], 7, None, ALU.arith_shift_right))
            link(dve.tensor_copy(slot_tile, slot_i[:, :, :].rearrange("p k b -> p (k b)")))
            dve.tensor_copy(signed_no[:, 0:NB], node_no[:, :])
            link(dve.tensor_scalar(signed_no[:, NB:2 * NB], node_no[:, :], -1.0, None, ALU.mult))

            def pick(i, s):
                m0 = LM * LS * i + LM * s
                dve.wait_ge(picked[s], i + 1)
                dve.tensor_tensor(hots[s], iota[:, :].unsqueeze(1).broadcast_to([P, LM, P]),
                                  slot_row[:, bass.ds(m0, LM)].unsqueeze(2).broadcast_to([P, LM, P]), ALU.is_equal)
                dve.tensor_tensor(picks[s], iota[:, 0:NJ].unsqueeze(1).broadcast_to([P, LM, NJ]),
                                  slot_tile[:, bass.ds(m0, LM)].unsqueeze(2).broadcast_to([P, LM, NJ]),
                                  ALU.is_equal).then_inc(hots_ready[s], 1)

            dve.wait_ge(table_out, 16 * LC_N)
            lists_steps(dve, pick)
            dve.wait_ge(x1_out, 16 * (LC_N + 1))
            link(dve.tensor_tensor(reach, iota[0:1, 0:NJ].unsqueeze(2).broadcast_to([1, NJ, NE]),
                                   tiles_c[0:1, :].unsqueeze(1).broadcast_to([1, NJ, NE]), ALU.is_ge))
            link(dve.tensor_reduce(expert_f, reach, AX.X, ALU.add))
            per_round = expert_f.rearrange("p (i s) -> p i s", s=XS)
            link(dve.memset(experts[:, 0, :], 0))
            dve.tensor_scalar(experts[:, :, 1:XS + 1], per_round, float(NE - 1), None, ALU.min)
            link(dve.tensor_scalar(experts[:, 1:, 0], per_round[:, 0:NJ // XS - 1, XS - 1], float(NE - 1), None, ALU.min))
            dve.wait_ge(lists_summed, 1)
            link(dve.tensor_scalar(of_choice[:, :, 1], bank[4][:, 0:NJ], 0.0, None, ALU.is_lt))
            link(dve.tensor_scalar(of_choice[:, :, 0], of_choice[:, :, 1], -1.0, 1.0, ALU.mult, ALU.add))
            link(dve.tensor_copy(is_empty, bank[4][:, 0:NJ]))
            link(dve.scalar_tensor_tensor(out=of_slot, in0=is_empty, scalar=-1.0, in1=is_empty, op0=ALU.mult, op1=ALU.max))
            link(dve.tensor_scalar(is_empty, of_slot, 0.0, None, ALU.is_equal))
            link(dve.scalar_tensor_tensor(out=of_slot, in0=is_empty, scalar=empty_no[:, 0:1], in1=of_slot, op0=ALU.mult, op1=ALU.add))
            dve.tensor_scalar(node_i, of_slot, -1.0, None, ALU.add).then_inc(lists_ready, 1)

            dve.wait_ge(w1_in, 16 * (DK + 1))
            dve.wait_ge(b2_in, 16)

            def rows_turned(j, s):
                dve.wait_ge(t_done, j + 1)
                for k in range(DK):
                    last = dve.tensor_scalar(xt[s][:, k, :], bank[0][:, k * P:(k + 1) * P], gb_sb[:, 0, k:k + 1],
                                             gb_sb[:, 1, k:k + 1], ALU.mult, ALU.add)
                last.then_inc(xt_ready, 1)
                if not isinstance(j, int) or j >= XS:
                    dve.wait_ge(y_ready, j - XS + 1)
                dve.tensor_tensor(weight[s][:, :], row[s][:, D:R],
                                  of_choice[:, bass.ds(j, 1), :].rearrange("p o k -> p (o k)"), ALU.mult).then_inc(row_free, 1)

            def hidden_bias(j, s, e):
                dve.wait_ge(h_done, j + 1)
                if not isinstance(j, int) or j >= XS:
                    dve.wait_ge(y_done, j - XS + 1)
                dve.tensor_tensor(hid[s], bank[1][:, :].rearrange("p (k t) -> p k t", k=HK),
                                  b1_sb[:, bass.ds(e, 1), :].rearrange("p o k -> p (o k)").unsqueeze(2).broadcast_to([P, HK, P]),
                                  ALU.add).then_inc(h_biased, 1)

            def weighted(j, s, e):
                dve.wait_ge(row_free, j + 1)
                dve.tensor_tensor(weight[s][:, 0:1], weight[s][:, 0:1], weight[s][:, 1:2], ALU.add).then_inc(weight_set, 1)
                dve.wait_ge(y_done, j + 1)
                if not isinstance(j, int) or j >= XS:
                    dve.wait_ge(y_free, j - XS + 1)
                dve.tensor_tensor(y_out[s], bank[3][:, 0:D], b2_sb[:, bass.ds(e, 1), :].rearrange("p o d -> p (o d)"),
                                  ALU.add).then_inc(y_biased, 1)
                dve.wait_ge(y_biased, j + 1)
                dve.wait_ge(weight_set, j + 1)
                dve.tensor_scalar(y_out[s], y_out[s], weight[s][:, 0:1], None, ALU.mult).then_inc(y_ready, 1)

            def dve_step(j, s, e):
                rows_turned(j + 1, (s + 1) % XS)
                hidden_bias(j, s, e[s + 1])
                weighted(j - 1, (s - 1) % XS, e[s])

            def dve_experts(i):
                return load_values(mybir.EngineType.DVE, experts[0:1, bass.ds(i, 1), :].rearrange("p o s -> p (o s)"), NE - 1, **unchecked)

            e = dve_experts(0)
            rows_turned(0, 0)
            rows_turned(1, 1)
            hidden_bias(0, 0, e[1])
            for j in range(1, XS):
                dve_step(j, j, e)
            e = dve_experts(1)
            for j in range(XS, 2 * XS):
                dve_step(j, j % XS, e)
            with dve.Fori(2, NJ // XS - 1) as i:
                rows_turned(XS * i + 1, 1)
                e = dve_experts(i)
                for s in range(XS):
                    if s:
                        rows_turned(XS * i + s + 1, (s + 1) % XS)
                    hidden_bias(XS * i + s, s, e[s + 1])
                    weighted(XS * i + s - 1, (s - 1) % XS, e[s])
            e = dve_experts(NJ // XS - 1)
            for j in range(NJ - XS, NJ - 1):
                dve_step(j, j % XS, e)
            hidden_bias(NJ - 1, (NJ - 1) % XS, e[XS])
            weighted(NJ - 2, (NJ - 2) % XS, e[XS - 1])
            weighted(NJ - 1, (NJ - 1) % XS, e[XS])


def kernel(x, src, dst, L0_gnn_W_self, L0_gnn_W_neigh, L0_gnn_b, L0_ffn_gamma, L0_ffn_beta, L0_ffn_Wr, L0_ffn_br,
           L0_ffn_W1, L0_ffn_b1, L0_ffn_W2, L0_ffn_b2):
    import numpy as np
    import concourse.bacc as bacc
    from concourse.bass_utils import run_bass_kernel_spmd

    n, d = x.shape
    lc = LC * P
    n_pad = -(-n // lc) * lc
    e_pad = -(-len(src) // (P * GT * GS)) * (P * GT * GS)

    def columns(a, fill):
        whole = np.full(e_pad, fill, a.dtype)
        whole[:len(a)] = a
        return np.ascontiguousarray(whole.reshape(-1, P).T)

    x_pad = np.zeros((n_pad, d), x.dtype)
    x_pad[:n] = x
    arrays = {
        "x": x_pad, "src": columns(np.asarray(src), 0), "dst": columns(np.asarray(dst), n_pad - 1),
        "w_self": L0_gnn_W_self, "w_neigh": L0_gnn_W_neigh, "b_gnn": np.reshape(L0_gnn_b, (1, -1)),
        "gamma": np.reshape(L0_ffn_gamma, (-1, P)).T, "beta": np.reshape(L0_ffn_beta, (-1, P)).T,
        "w_r": L0_ffn_Wr, "b_r": np.reshape(L0_ffn_br, (1, -1)),
        "w1": L0_ffn_W1, "b1": np.reshape(L0_ffn_b1, (len(L0_ffn_b1), -1, P)).transpose(2, 0, 1), "w2": L0_ffn_W2, "b2": np.reshape(L0_ffn_b2, (1, -1)),
    }
    nc = bacc.Bacc("TRN2", target_bir_lowering=False, num_devices=1)
    feeds, args = {}, {}
    for name, a in arrays.items():
        a = np.ascontiguousarray(a)
        feeds[f"in_{name}"] = a
        args[name] = nc.dram_tensor(f"in_{name}", a.shape, mybir.dt.from_np(a.dtype), kind="ExternalInput").ap()
    out = nc.dram_tensor("out", (n_pad + P, d), F32, kind="ExternalOutput").ap()
    build(nc, out=out, **args)
    got = run_bass_kernel_spmd(nc, [feeds], core_ids=[0]).results[0]["out"]
    return got[:n]
```
